# Optimizing a Trainium2 kernel written in Bass

```python
import numpy as np
import jax
import jax.numpy as jnp

def _softmax(x, axis=-1):
    return jax.nn.softmax(x, axis=axis)

def _gelu(x):
    return jax.nn.gelu(x, approximate=True)

def _silu(x):
    return jax.nn.silu(x)

def _sigmoid(x):
    return jax.nn.sigmoid(x)

def _layernorm(x, axis=-1, eps=1e-05):
    m = jnp.mean(x, axis=axis, keepdims=True)
    v = jnp.var(x, axis=axis, keepdims=True)
    return (x - m) / jnp.sqrt(v + eps)

def _scatter_add(tgt, idx, src, axis=0):
    return tgt.at[idx].add(src)

def _segment_sum(src, seg, n):
    return jax.ops.segment_sum(src, seg, n)
kernel_name = 'mk_dlrm_tower_d1_rec_r8_a4b44a'

def setup_inputs(seed: int=0):
    np.random.seed(seed)
    _w = jnp.asarray

    def _rec_inputs():
        import jax
        import jax.numpy as jnp
        _tk = jax.random.key(seed)
        dense_ctx = jax.random.normal(jax.random.fold_in(_tk, 190), (512, 16), jnp.float32)
        ids = jnp.stack([jax.random.randint(jax.random.fold_in(_tk, 200 + f), (512,), 0, v, jnp.int32) for f, v in enumerate([1000, 12500, 1250, 12500, 12500, 1000, 1250, 1000, 125000, 125000, 12500, 12500, 125000, 1250, 1250, 12500, 125000, 1250, 12500, 12500, 1250, 1250, 1000, 1000, 1250, 12500, 1000, 1250, 125000, 1000, 1000, 12500])], axis=1)
        tbl_0 = 0.05 * jax.random.normal(jax.random.fold_in(_tk, 500 + 0), (1000, 16), jnp.float32)
        tbl_1 = 0.05 * jax.random.normal(jax.random.fold_in(_tk, 500 + 1), (12500, 16), jnp.float32)
        tbl_2 = 0.05 * jax.random.normal(jax.random.fold_in(_tk, 500 + 2), (1250, 16), jnp.float32)
        tbl_3 = 0.05 * jax.random.normal(jax.random.fold_in(_tk, 500 + 3), (12500, 16), jnp.float32)
        tbl_4 = 0.05 * jax.random.normal(jax.random.fold_in(_tk, 500 + 4), (12500, 16), jnp.float32)
        tbl_5 = 0.05 * jax.random.normal(jax.random.fold_in(_tk, 500 + 5), (1000, 16), jnp.float32)
        tbl_6 = 0.05 * jax.random.normal(jax.random.fold_in(_tk, 500 + 6), (1250, 16), jnp.float32)
        tbl_7 = 0.05 * jax.random.normal(jax.random.fold_in(_tk, 500 + 7), (1000, 16), jnp.float32)
        tbl_8 = 0.05 * jax.random.normal(jax.random.fold_in(_tk, 500 + 8), (125000, 16), jnp.float32)
        tbl_9 = 0.05 * jax.random.normal(jax.random.fold_in(_tk, 500 + 9), (125000, 16), jnp.float32)
        tbl_10 = 0.05 * jax.random.normal(jax.random.fold_in(_tk, 500 + 10), (12500, 16), jnp.float32)
        tbl_11 = 0.05 * jax.random.normal(jax.random.fold_in(_tk, 500 + 11), (12500, 16), jnp.float32)
        tbl_12 = 0.05 * jax.random.normal(jax.random.fold_in(_tk, 500 + 12), (125000, 16), jnp.float32)
        tbl_13 = 0.05 * jax.random.normal(jax.random.fold_in(_tk, 500 + 13), (1250, 16), jnp.float32)
        tbl_14 = 0.05 * jax.random.normal(jax.random.fold_in(_tk, 500 + 14), (1250, 16), jnp.float32)
        tbl_15 = 0.05 * jax.random.normal(jax.random.fold_in(_tk, 500 + 15), (12500, 16), jnp.float32)
        tbl_16 = 0.05 * jax.random.normal(jax.random.fold_in(_tk, 500 + 16), (125000, 16), jnp.float32)
        tbl_17 = 0.05 * jax.random.normal(jax.random.fold_in(_tk, 500 + 17), (1250, 16), jnp.float32)
        tbl_18 = 0.05 * jax.random.normal(jax.random.fold_in(_tk, 500 + 18), (12500, 16), jnp.float32)
        tbl_19 = 0.05 * jax.random.normal(jax.random.fold_in(_tk, 500 + 19), (12500, 16), jnp.float32)
        tbl_20 = 0.05 * jax.random.normal(jax.random.fold_in(_tk, 500 + 20), (1250, 16), jnp.float32)
        tbl_21 = 0.05 * jax.random.normal(jax.random.fold_in(_tk, 500 + 21), (1250, 16), jnp.float32)
        tbl_22 = 0.05 * jax.random.normal(jax.random.fold_in(_tk, 500 + 22), (1000, 16), jnp.float32)
        tbl_23 = 0.05 * jax.random.normal(jax.random.fold_in(_tk, 500 + 23), (1000, 16), jnp.float32)
        tbl_24 = 0.05 * jax.random.normal(jax.random.fold_in(_tk, 500 + 24), (1250, 16), jnp.float32)
        tbl_25 = 0.05 * jax.random.normal(jax.random.fold_in(_tk, 500 + 25), (12500, 16), jnp.float32)
        tbl_26 = 0.05 * jax.random.normal(jax.random.fold_in(_tk, 500 + 26), (1000, 16), jnp.float32)
        tbl_27 = 0.05 * jax.random.normal(jax.random.fold_in(_tk, 500 + 27), (1250, 16), jnp.float32)
        tbl_28 = 0.05 * jax.random.normal(jax.random.fold_in(_tk, 500 + 28), (125000, 16), jnp.float32)
        tbl_29 = 0.05 * jax.random.normal(jax.random.fold_in(_tk, 500 + 29), (1000, 16), jnp.float32)
        tbl_30 = 0.05 * jax.random.normal(jax.random.fold_in(_tk, 500 + 30), (1000, 16), jnp.float32)
        tbl_31 = 0.05 * jax.random.normal(jax.random.fold_in(_tk, 500 + 31), (12500, 16), jnp.float32)
        _rk = jax.random.fold_in(_tk, 7)
        W_top1 = 0.0606339 * jax.random.normal(jax.random.fold_in(_tk, 801), (272, 512), jnp.float32)
        W_top2 = 0.0441942 * jax.random.normal(jax.random.fold_in(_tk, 802), (512, 256), jnp.float32)
        W_top3 = 0.0625 * jax.random.normal(jax.random.fold_in(_tk, 803), (256, 1), jnp.float32)
        b_top1 = jnp.zeros((512,), jnp.float32)
        b_top2 = jnp.zeros((256,), jnp.float32)
        return (dense_ctx, ids, tbl_0, tbl_1, tbl_2, tbl_3, tbl_4, tbl_5, tbl_6, tbl_7, tbl_8, tbl_9, tbl_10, tbl_11, tbl_12, tbl_13, tbl_14, tbl_15, tbl_16, tbl_17, tbl_18, tbl_19, tbl_20, tbl_21, tbl_22, tbl_23, tbl_24, tbl_25, tbl_26, tbl_27, tbl_28, tbl_29, tbl_30, tbl_31, W_top1, b_top1, W_top2, b_top2, W_top3)
    dense_ctx, ids, tbl_0, tbl_1, tbl_2, tbl_3, tbl_4, tbl_5, tbl_6, tbl_7, tbl_8, tbl_9, tbl_10, tbl_11, tbl_12, tbl_13, tbl_14, tbl_15, tbl_16, tbl_17, tbl_18, tbl_19, tbl_20, tbl_21, tbl_22, tbl_23, tbl_24, tbl_25, tbl_26, tbl_27, tbl_28, tbl_29, tbl_30, tbl_31, W_top1, b_top1, W_top2, b_top2, W_top3 = _rec_inputs()

    def _L0_rec_setup():
        import jax, jax.numpy as jnp
        import numpy as np
        NUM_FIELDS = 32
        EMBED_DIM = 16
        BATCH = 512
        CROSS_SIZES = [128, 128, 128]

        def _cin_forward(x, Ws, bs):
            x0 = x
            h = x
            xs = []
            n_layers = len(Ws)
            for i in range(n_layers):
                B, F, E = x0.shape
                G = h.shape[1]
                z = (x0[:, :, None, :] * h[:, None, :, :]).reshape(B, F * G, E)
                y = jax.nn.relu(jnp.einsum('oc,bce->boe', Ws[i], z) + bs[i][None, :, None])
                if i != n_layers - 1:
                    half = y.shape[1] // 2
                    x_keep, h = (y[:, :half, :], y[:, half:, :])
                else:
                    x_keep, h = (y, y)
                xs.append(x_keep)
            return jnp.sum(jnp.concatenate(xs, axis=1), axis=2)
        key = jax.random.key(seed)
        ks = jax.random.split(key, 8)
        x = jax.random.normal(ks[0], (BATCH, NUM_FIELDS, EMBED_DIM), dtype=jnp.float32)
        prev = NUM_FIELDS
        inp = {'x': x}
        for i, cs in enumerate(CROSS_SIZES):
            in_ch = NUM_FIELDS * prev
            scale = 1.0 / np.sqrt(in_ch)
            inp[f'W{i}'] = jax.random.uniform(ks[1 + 2 * i], (cs, in_ch), dtype=jnp.float32, minval=-scale, maxval=scale)
            inp[f'b{i}'] = jax.random.uniform(ks[2 + 2 * i], (cs,), dtype=jnp.float32, minval=-scale, maxval=scale)
            prev = cs // 2
        return inp
    _L0_rec_all = _L0_rec_setup()
    _L0_rec_in = {k: v for k, v in _L0_rec_all.items() if k in ('W0', 'b0', 'W1', 'b1', 'W2', 'b2')}
    del _L0_rec_all
    return {'dense_ctx': dense_ctx, 'ids': ids, 'tbl_0': tbl_0, 'tbl_1': tbl_1, 'tbl_2': tbl_2, 'tbl_3': tbl_3, 'tbl_4': tbl_4, 'tbl_5': tbl_5, 'tbl_6': tbl_6, 'tbl_7': tbl_7, 'tbl_8': tbl_8, 'tbl_9': tbl_9, 'tbl_10': tbl_10, 'tbl_11': tbl_11, 'tbl_12': tbl_12, 'tbl_13': tbl_13, 'tbl_14': tbl_14, 'tbl_15': tbl_15, 'tbl_16': tbl_16, 'tbl_17': tbl_17, 'tbl_18': tbl_18, 'tbl_19': tbl_19, 'tbl_20': tbl_20, 'tbl_21': tbl_21, 'tbl_22': tbl_22, 'tbl_23': tbl_23, 'tbl_24': tbl_24, 'tbl_25': tbl_25, 'tbl_26': tbl_26, 'tbl_27': tbl_27, 'tbl_28': tbl_28, 'tbl_29': tbl_29, 'tbl_30': tbl_30, 'tbl_31': tbl_31, 'W_top1': W_top1, 'b_top1': b_top1, 'W_top2': W_top2, 'b_top2': b_top2, 'W_top3': W_top3, 'L0_rec_W0': _L0_rec_in['W0'], 'L0_rec_b0': _L0_rec_in['b0'], 'L0_rec_W1': _L0_rec_in['W1'], 'L0_rec_b1': _L0_rec_in['b1'], 'L0_rec_W2': _L0_rec_in['W2'], 'L0_rec_b2': _L0_rec_in['b2']}

def reference(dense_ctx, ids, tbl_0, tbl_1, tbl_2, tbl_3, tbl_4, tbl_5, tbl_6, tbl_7, tbl_8, tbl_9, tbl_10, tbl_11, tbl_12, tbl_13, tbl_14, tbl_15, tbl_16, tbl_17, tbl_18, tbl_19, tbl_20, tbl_21, tbl_22, tbl_23, tbl_24, tbl_25, tbl_26, tbl_27, tbl_28, tbl_29, tbl_30, tbl_31, W_top1, b_top1, W_top2, b_top2, W_top3, L0_rec_W0, L0_rec_b0, L0_rec_W1, L0_rec_b1, L0_rec_W2, L0_rec_b2):
    import jax
    import jax.numpy as jnp

    def _L0_rec_ref(x, W0, b0, W1, b1, W2, b2):
        import jax, jax.numpy as jnp
        import numpy as np
        NUM_FIELDS = 32
        EMBED_DIM = 16
        BATCH = 512
        CROSS_SIZES = [128, 128, 128]

        def _cin_forward(x, Ws, bs):
            x0 = x
            h = x
            xs = []
            n_layers = len(Ws)
            for i in range(n_layers):
                B, F, E = x0.shape
                G = h.shape[1]
                z = (x0[:, :, None, :] * h[:, None, :, :]).reshape(B, F * G, E)
                y = jax.nn.relu(jnp.einsum('oc,bce->boe', Ws[i], z) + bs[i][None, :, None])
                if i != n_layers - 1:
                    half = y.shape[1] // 2
                    x_keep, h = (y[:, :half, :], y[:, half:, :])
                else:
                    x_keep, h = (y, y)
                xs.append(x_keep)
            return jnp.sum(jnp.concatenate(xs, axis=1), axis=2)
        return _cin_forward(x, [W0, W1, W2], [b0, b1, b2])
    e = jnp.stack([tbl_0[ids[:, 0]], tbl_1[ids[:, 1]], tbl_2[ids[:, 2]], tbl_3[ids[:, 3]], tbl_4[ids[:, 4]], tbl_5[ids[:, 5]], tbl_6[ids[:, 6]], tbl_7[ids[:, 7]], tbl_8[ids[:, 8]], tbl_9[ids[:, 9]], tbl_10[ids[:, 10]], tbl_11[ids[:, 11]], tbl_12[ids[:, 12]], tbl_13[ids[:, 13]], tbl_14[ids[:, 14]], tbl_15[ids[:, 15]], tbl_16[ids[:, 16]], tbl_17[ids[:, 17]], tbl_18[ids[:, 18]], tbl_19[ids[:, 19]], tbl_20[ids[:, 20]], tbl_21[ids[:, 21]], tbl_22[ids[:, 22]], tbl_23[ids[:, 23]], tbl_24[ids[:, 24]], tbl_25[ids[:, 25]], tbl_26[ids[:, 26]], tbl_27[ids[:, 27]], tbl_28[ids[:, 28]], tbl_29[ids[:, 29]], tbl_30[ids[:, 30]], tbl_31[ids[:, 31]]], axis=1)
    z = _L0_rec_ref(e, L0_rec_W0, L0_rec_b0, L0_rec_W1, L0_rec_b1, L0_rec_W2, L0_rec_b2)
    z = z.reshape(z.shape[0], -1)
    h = jnp.concatenate([z, dense_ctx], axis=1)
    h = jnp.maximum(h @ W_top1 + b_top1, 0.0)
    h = jnp.maximum(h @ W_top2 + b_top2, 0.0)
    y = h @ W_top3
    return y

_drawn_inputs = setup_inputs


def setup_inputs(seed=0):
    import zlib

    import numpy as np

    out = dict(_drawn_inputs(seed))
    spreads = {'b_top1': (0.0, 0.357), 'b_top2': (0.0, 0.408)}
    factors = {'tbl_0': 8.0,
     'tbl_1': 8.0,
     'tbl_2': 8.0,
     'tbl_3': 8.0,
     'tbl_4': 8.0,
     'tbl_5': 8.0,
     'tbl_6': 8.0,
     'tbl_7': 8.0,
     'tbl_8': 8.0,
     'tbl_9': 8.0,
     'tbl_10': 8.0,
     'tbl_11': 8.0,
     'tbl_12': 8.0,
     'tbl_13': 8.0,
     'tbl_14': 8.0,
     'tbl_15': 8.0,
     'tbl_16': 8.0,
     'tbl_17': 8.0,
     'tbl_18': 8.0,
     'tbl_19': 8.0,
     'tbl_20': 8.0,
     'tbl_21': 8.0,
     'tbl_22': 8.0,
     'tbl_23': 8.0,
     'tbl_24': 8.0,
     'tbl_25': 8.0,
     'tbl_26': 8.0,
     'tbl_27': 8.0,
     'tbl_28': 8.0,
     'tbl_29': 8.0,
     'tbl_30': 8.0,
     'tbl_31': 8.0,
     'L0_rec_W0': 8.0,
     'L0_rec_W1': 8.0,
     'L0_rec_W2': 8.0,
     'L0_rec_b0': 4.919,
     'L0_rec_b1': 6.997,
     'L0_rec_b2': 7.302}
    for name, (base, spread) in spreads.items():
        noise = np.random.default_rng([zlib.crc32(name.encode()), seed]).standard_normal(out[name].shape)
        drawn = base * np.exp(spread * noise) if base else spread * noise
        out[name] = jnp.asarray(drawn.astype(out[name].dtype))
    for name, factor in factors.items():
        out[name] = (out[name] * factor).astype(out[name].dtype)
    return out
```

```python
from contextlib import ExitStack

import concourse.bass as bass
from concourse import mybir

F32 = mybir.dt.float32
I32 = mybir.dt.int32
ALU = mybir.AluOpType
ACT = mybir.ActivationFunctionType
AX_X = mybir.AxisListType.X

P = 128
FIELDS = 32
EMB = 16
HALF = 64
COLS = 512
SAMPLES = COLS // EMB
SPLIT = P // FIELDS
LOOKUPS = SAMPLES // SPLIT
DIAGS = FIELDS // 2 + 1
PAIR_TILES = (DIAGS - 1) // SPLIT
CROSS_TILES = FIELDS * HALF // P
GROUP = 4
CROSS_GROUPS = CROSS_TILES // GROUP
FIRST_GROUPS = 2
STAGE_GROUPS = 2 * CROSS_GROUPS + FIRST_GROUPS
RING = 5
assert STAGE_GROUPS % RING == 0


def cin_tower(nc, ids, offsets, table, w0a, w0b, w1, w2, biases, dense,
              top1, top1_bias, top2, top2_bias, top3, out):
    chunks = ids.shape[1] // LOOKUPS
    batch = chunks * SAMPLES
    hidden1 = top1.shape[1]
    hidden2 = top2.shape[2]
    tiles1 = hidden1 // P
    tiles2 = hidden2 // P
    assert chunks % 2 == 0 and chunks >= 4 and batch <= 512

    x0_dram = nc.dram_tensor("x0_rows", (chunks, 2 * FIELDS, COLS), F32, kind="Internal").ap()

    with ExitStack() as ctx:
        def sb(name, shape, dt=F32):
            return ctx.enter_context(nc.sbuf_tensor(name, shape, dt))

        def bank(name):
            return ctx.enter_context(nc.psum_tensor(name, [P, COLS], F32))

        def sem(name):
            return ctx.enter_context(nc.semaphore(name))

        idx_local = sb("idx_local", [P, chunks * LOOKUPS], I32)
        idx_offset = sb("idx_offset", [P, LOOKUPS], I32)
        idx = sb("idx", [P, 2, LOOKUPS], I32)
        gathered = sb("gathered", [P, 2, LOOKUPS * EMB])
        rot = sb("rot", [P, 2, PAIR_TILES + 2, COLS])
        xrep = sb("xrep", [P, 2, CROSS_TILES, COLS])
        z = sb("z", [P, RING, GROUP, COLS])
        h = [sb("h0", [P, COLS]), sb("h1", [P, COLS])]
        kept = [sb("kept0", [HALF, COLS]), sb("kept1", [HALF, COLS]), sb("kept2", [P, COLS])]
        w0_sb = sb("w0_sb", [P, PAIR_TILES + 1, P])
        w0b_sb = sb("w0b_sb", [P, PAIR_TILES, P])
        w_sb = [None, sb("w1_sb", [P, CROSS_TILES, P]), sb("w2_sb", [P, CROSS_TILES, P])]
        bias_sb = sb("bias_sb", [P, 3])
        sums01 = sb("sums01", [P, batch])
        sums2 = sb("sums2", [P, batch])
        dense_sb = sb("dense_sb", [EMB, batch])
        top1_sb = sb("top1_sb", [P, 2, hidden1])
        top1d_sb = sb("top1d_sb", [EMB, hidden1])
        top1_bias_sb = sb("top1_bias_sb", [P, tiles1])
        top2_sb = sb("top2_sb", [P, tiles1, hidden2])
        top2_bias_sb = sb("top2_bias_sb", [P, tiles2])
        top3_sb = sb("top3_sb", [P, tiles2])
        hid1 = sb("hid1", [P, tiles1, batch])
        hid2 = sb("hid2", [P, tiles2, batch])
        out_sb = sb("out_sb", [1, batch])

        y = [bank("y0"), bank("y1"), bank("y2")]
        mlp = [bank(f"mlp{i}") for i in range(4)]

        ids_loaded = sem("ids_loaded")
        w0_loaded = sem("w0_loaded")
        w1_loaded = sem("w1_loaded")
        w2_loaded = sem("w2_loaded")
        bias_loaded = sem("bias_loaded")
        top_loaded = sem("top_loaded")
        idx_ready = sem("idx_ready")
        pool_steps = sem("pool_steps")
        rows_gathered = [sem("rows_gathered_a"), sem("rows_gathered_b")]
        x0_stored = [sem("x0_stored_a"), sem("x0_stored_b")]
        rot_loaded = [sem("rot_loaded_a"), sem("rot_loaded_b")]
        xrep_loaded = [sem("xrep_loaded_a"), sem("xrep_loaded_b")]
        w0_folded = sem("w0_folded")
        z_made = sem("z_made")
        z_used = sem("z_used")
        h_ready = [sem("h0_ready"), sem("h1_ready")]
        kept_ready = [sem("kept0_ready"), sem("kept1_ready"), sem("kept2_ready")]
        kept_summed = [sem("kept0_summed"), sem("kept1_summed"), sem("kept2_summed")]
        hid1_acc = sem("hid1_acc")
        hid1_ready = sem("hid1_ready")
        hid2_acc = sem("hid2_acc")
        hid2_ready = sem("hid2_ready")
        score_acc = sem("score_acc")
        score_ready = sem("score_ready")
        out_stored = sem("out_stored")

        def layer1_group(c, k):
            return FIRST_GROUPS + STAGE_GROUPS * c + k

        def layer0_group(c, k):
            if isinstance(c, int) and c == 0:
                return k
            return STAGE_GROUPS * (c - 1) + FIRST_GROUPS + CROSS_GROUPS + k

        def layer2_group(c, k):
            if isinstance(c, int) and c == chunks - 1:
                return FIRST_GROUPS + STAGE_GROUPS * c + CROSS_GROUPS + k
            return FIRST_GROUPS + STAGE_GROUPS * c + CROSS_GROUPS + FIRST_GROUPS + k

        def slot0(c, k):
            return (k if isinstance(c, int) and c == 0 else FIRST_GROUPS + CROSS_GROUPS + k) % RING

        def slot12(layer, c, k):
            after = layer == 2 and not (isinstance(c, int) and c == chunks - 1)
            return (FIRST_GROUPS + (layer - 1) * CROSS_GROUPS + after * FIRST_GROUPS + k) % RING

        def cross_group(layer, c, k):
            return layer1_group(c, k) if layer == 1 else layer2_group(c, k)

        ROT_DMAS = 2 * SPLIT
        REP_DMAS = 2
        TOP_DMAS = 7

        def over_chunks(eng, pair):
            pair(0, 1, True, False)
            if chunks > 4:
                with eng.Fori(1, chunks // 2 - 1) as i:
                    pair(2 * i, i + 1, False, False)
            pair(chunks - 2, chunks // 2, False, True)

        block = ctx.enter_context(nc.Block())

        @block.sync
        def _(sp):
            sp.dma_start(idx_local[:], ids).then_inc(ids_loaded, 16)
            sp.dma_start(idx_offset[:], offsets).then_inc(ids_loaded, 16)
            sp.dma_start(w0_sb[:, 0:PAIR_TILES, :], w0a[:, 0:PAIR_TILES, :]).then_inc(w0_loaded, 16)
            sp.dma_start(w0_sb[0:FIELDS, PAIR_TILES, :], w0a[0:FIELDS, PAIR_TILES, :]).then_inc(w0_loaded, 16)
            sp.dma_start(w0b_sb[:], w0b).then_inc(w0_loaded, 16)
            sp.dma_start(bias_sb[:], biases).then_inc(bias_loaded, 16)

            def store_x0(c, u, n):
                sp.wait_ge(rows_gathered[u], 16 * LOOKUPS * n)
                rows = x0_dram[c].rearrange("(two f) (s n) -> two (f s) n", two=2, s=SPLIT)
                for copy in range(2):
                    sp.dma_start(rows[copy], gathered[:, u, :]).then_inc(x0_stored[u], 16)

            def load_rot(c, u, n, first):
                sp.wait_ge(x0_stored[u], 32 * n)
                if not first:
                    sp.wait_ge(z_made, layer1_group(c - 2, 1))
                for k in range(SPLIT):
                    rows = slice(FIELDS * k, FIELDS * (k + 1))
                    sp.dma_start(rot[rows, u, 0, :], x0_dram[c][0:FIELDS, :]).then_inc(rot_loaded[u], 16)
                    tiles = PAIR_TILES + 1 if k == 0 else PAIR_TILES
                    win = x0_dram[c][k:k + FIELDS, :]
                    src = bass.AP(tensor=win.tensor, offset=win.offset,
                                  ap=[[COLS, FIELDS], [SPLIT * COLS, tiles], [1, COLS]])
                    sp.dma_start(rot[rows, u, 1:1 + tiles, :], src).then_inc(rot_loaded[u], 16)

            def load_xrep(c, u, n, first):
                if not first:
                    sp.wait_ge(z_made, layer2_group(c - 2, CROSS_GROUPS))
                for half in range(2):
                    win = x0_dram[c][half:half + 1, :]
                    src = bass.AP(tensor=win.tensor, offset=win.offset,
                                  ap=[[0, HALF], [2 * COLS, CROSS_TILES], [1, COLS]])
                    sp.dma_start(xrep[HALF * half:HALF * (half + 1), u, :, :], src).then_inc(xrep_loaded[u], 16)

            def pair(c, n, first, last):
                for u in range(2):
                    store_x0(c + u, u, n)
                    load_rot(c + u, u, n, first)
                    load_xrep(c + u, u, n, first)
                    if first and u == 0:
                        sp.dma_start(w_sb[1][:], w1).then_inc(w1_loaded, 16)
                        sp.dma_start(w_sb[2][:], w2).then_inc(w2_loaded, 16)

            over_chunks(sp, pair)
            sp.dma_start(dense_sb[:], dense).then_inc(top_loaded, 16)
            sp.dma_start(top1_sb[:], top1[0:2 * P, :].rearrange("(t p) n -> p t n", t=2)).then_inc(top_loaded, 16)
            sp.dma_start(top1d_sb[:], top1[2 * P:2 * P + EMB, :]).then_inc(top_loaded, 16)
            sp.dma_start(top1_bias_sb[:], top1_bias).then_inc(top_loaded, 16)
            sp.dma_start(top2_sb[:], top2).then_inc(top_loaded, 16)
            sp.dma_start(top2_bias_sb[:], top2_bias).then_inc(top_loaded, 16)
            sp.dma_start(top3_sb[:], top3).then_inc(top_loaded, 16)
            sp.wait_ge(score_ready, 1)
            sp.dma_start(out, out_sb[:]).then_inc(out_stored, 16)
            sp.wait_ge(out_stored, 16)

        @block.gpsimd
        def _(pool):
            def pair(c, n, first, last):
                for u in range(2):
                    if not first:
                        pool.wait_ge(x0_stored[u], 32 * (n - 1))
                        pool.sem_inc(pool_steps, 1)
                    pool.wait_ge(ids_loaded, 32)
                    nc.gpsimd.tensor_tensor(out=idx[:, u, :],
                                            in0=idx_local[:, bass.ds((c + u) * LOOKUPS, LOOKUPS)],
                                            in1=idx_offset[:], op=ALU.add).then_inc(idx_ready, 1)
                    pool.wait_ge(idx_ready, c + u + 1)
                    pool.sem_inc(pool_steps, 1)
                    for q in range(LOOKUPS):
                        nc.gpsimd.indirect_dma_start(
                            out=gathered[:, u, q * EMB:(q + 1) * EMB], out_offset=None, in_=table,
                            in_offset=bass.IndirectOffsetOnAxis(ap=idx[:, u, q:q + 1], axis=0),
                        ).then_inc(rows_gathered[u], 16)

            over_chunks(pool, pair)

        @block.vector
        def _(dve):
            dve.wait_ge(w0_loaded, 48)
            for lo, hi in ((FIELDS, HALF), (HALF, P)):
                nc.vector.tensor_tensor(out=w0_sb[lo:hi, 0, :], in0=w0_sb[lo:hi, 0, :],
                                        in1=w0b_sb[lo:hi, 0, :], op=ALU.add).then_inc(w0_folded, 1)
            nc.vector.tensor_tensor(out=w0_sb[:, 1:PAIR_TILES, :], in0=w0_sb[:, 1:PAIR_TILES, :],
                                    in1=w0b_sb[:, 1:, :], op=ALU.add).then_inc(w0_folded, 1)

            def wait_slot(group, early):
                if not early:
                    dve.wait_ge(z_used, group - RING + 1)

            def make_layer0(c, u, n, early=False):
                dve.wait_ge(rot_loaded[u], 16 * ROT_DMAS * n)
                wait_slot(layer0_group(c, 0), early)
                nc.vector.tensor_tensor(
                    out=z[:, slot0(c, 0), :, :],
                    in0=rot[:, u, 1:1 + PAIR_TILES, :],
                    in1=rot[:, u, 0:1, :].to_broadcast([P, PAIR_TILES, COLS]),
                    op=ALU.mult).then_inc(z_made, 1)
                wait_slot(layer0_group(c, 1), early)
                nc.vector.tensor_tensor(
                    out=z[0:FIELDS, slot0(c, 1), 0, :],
                    in0=rot[0:FIELDS, u, 1 + PAIR_TILES, :], in1=rot[0:FIELDS, u, 0, :],
                    op=ALU.mult).then_inc(z_made, 1)

            def make_cross(layer, c, u, k, early):
                wait_slot(cross_group(layer, c, k), early)
                nc.vector.tensor_tensor(
                    out=z[:, slot12(layer, c, k), :, :],
                    in0=xrep[:, u, k * GROUP:(k + 1) * GROUP, :],
                    in1=h[layer - 1][:].unsqueeze(1).to_broadcast([P, GROUP, COLS]),
                    op=ALU.mult).then_inc(z_made, 1)

            def sum_kept(layer, c):
                dve.wait_ge(kept_ready[layer], c + 1)
                rows = P if layer == 2 else HALF
                if layer == 2:
                    dst = sums2[:, bass.ds(c * SAMPLES, SAMPLES)]
                else:
                    dst = sums01[HALF * layer:HALF * (layer + 1), bass.ds(c * SAMPLES, SAMPLES)]
                nc.vector.tensor_reduce(out=dst, in_=kept[layer][0:rows, :].rearrange("p (s e) -> p s e", e=EMB),
                                        axis=AX_X, op=ALU.add).then_inc(kept_summed[layer], 1)

            def pair(c0, n, first, last):
                for u in range(2):
                    c = c0 + u
                    start = first and u == 0
                    end = last and u == 1
                    dve.wait_ge(xrep_loaded[u], 16 * REP_DMAS * n)
                    dve.wait_ge(h_ready[0], 2 * (c + 1))
                    for k in range(CROSS_GROUPS):
                        make_cross(1, c, u, k, early=start and FIRST_GROUPS + k < RING)
                    if not start:
                        sum_kept(2, c - 1)
                    if not end:
                        make_layer0(c + 1, 1 - u, n + u)
                    dve.wait_ge(h_ready[1], 2 * (c + 1))
                    for k in range(CROSS_GROUPS):
                        make_cross(2, c, u, k, early=False)
                        if k == 0:
                            sum_kept(1, c)
                    if not end:
                        sum_kept(0, c + 1)

            make_layer0(0, 0, 1, early=True)
            sum_kept(0, 0)
            over_chunks(dve, pair)
            sum_kept(2, chunks - 1)
            dve.wait_ge(score_acc, 1)
            nc.vector.tensor_copy(out_sb[:], y[2][0:1, 0:batch]).then_inc(score_ready, 1)

        @block.tensor
        def _(pe):
            def layer0(c, first=False):
                if not first:
                    pe.wait_ge(h_ready[0], 2 * c)
                    pe.wait_ge(kept_ready[0], c)
                pe.wait_ge(z_made, layer0_group(c, 0) + 1)
                for t in range(PAIR_TILES):
                    last = nc.tensor.matmul(y[0][:], w0_sb[:, t, :], z[:, slot0(c, 0), t, :],
                                            start=t == 0, stop=False)
                last.then_inc(z_used, 1)
                pe.wait_ge(z_made, layer0_group(c, 1) + 1)
                last = nc.tensor.matmul(y[0][:], w0_sb[0:FIELDS, PAIR_TILES, :],
                                        z[0:FIELDS, slot0(c, 1), 0, :], start=False, stop=True)
                last.then_inc(z_used, 1)

            def cross(layer, c, start=False):
                if not start:
                    if layer == 1:
                        pe.wait_ge(h_ready[1], 2 * c)
                    pe.wait_ge(kept_ready[layer], c)
                for k in range(CROSS_GROUPS):
                    pe.wait_ge(z_made, cross_group(layer, c, k) + 1)
                    for t in range(GROUP):
                        last = nc.tensor.matmul(y[layer][:], w_sb[layer][:, k * GROUP + t, :],
                                                z[:, slot12(layer, c, k), t, :],
                                                start=k + t == 0, stop=k == CROSS_GROUPS - 1 and t == GROUP - 1)
                    last.then_inc(z_used, 1)

            def pair(c0, n, first, last):
                for u in range(2):
                    c = c0 + u
                    start = first and u == 0
                    cross(1, c, start)
                    if not (last and u == 1):
                        layer0(c + 1)
                    cross(2, c, start)

            pe.wait_ge(w0_loaded, 48)
            pe.wait_ge(w0_folded, 3)
            layer0(0, first=True)
            pe.wait_ge(w1_loaded, 16)
            pe.wait_ge(w2_loaded, 16)
            over_chunks(pe, pair)

            pe.wait_ge(top_loaded, 16 * TOP_DMAS)
            for layer in range(3):
                pe.wait_ge(kept_summed[layer], chunks)
            for t in range(tiles1):
                cols = slice(P * t, P * (t + 1))
                nc.tensor.matmul(mlp[t][:, 0:batch], top1d_sb[:, cols], dense_sb[:], start=True, stop=False)
                nc.tensor.matmul(mlp[t][:, 0:batch], top1_sb[:, 0, cols], sums01[:], start=False, stop=False)
                nc.tensor.matmul(mlp[t][:, 0:batch], top1_sb[:, 1, cols], sums2[:],
                                 start=False, stop=True).then_inc(hid1_acc, 1)
            for t in range(tiles2):
                for k in range(tiles1):
                    pe.wait_ge(hid1_ready, k + 1)
                    last = nc.tensor.matmul(y[t][:, 0:batch], top2_sb[:, k, P * t:P * (t + 1)], hid1[:, k, :],
                                            start=k == 0, stop=k == tiles1 - 1)
                last.then_inc(hid2_acc, 1)
            for k in range(tiles2):
                pe.wait_ge(hid2_ready, k + 1)
                last = nc.tensor.matmul(y[2][0:1, 0:batch], top3_sb[:, k:k + 1], hid2[:, k, :],
                                        start=k == 0, stop=k == tiles2 - 1)
            last.then_inc(score_acc, 1)

        @block.scalar
        def _(act):
            def relu(dst, src, bias):
                return nc.scalar.activation(dst, src, ACT.Relu, bias=bias)

            def evacuate(layer, c, done, start):
                act.wait_ge(z_used, done)
                if layer == 2:
                    if not start:
                        act.wait_ge(kept_summed[2], c)
                    relu(kept[2][:], y[2][:], bias_sb[:, 2:3]).then_inc(kept_ready[2], 1)
                    return
                up = slice(HALF, P)
                relu(h[layer][up, :], y[layer][up, :], bias_sb[up, layer:layer + 1]).then_inc(h_ready[layer], 1)
                relu(h[layer][0:HALF, :], y[layer][up, :],
                     bias_sb[up, layer:layer + 1]).then_inc(h_ready[layer], 1)
                if not start:
                    act.wait_ge(kept_summed[layer], c)
                relu(kept[layer][:], y[layer][0:HALF, :],
                     bias_sb[0:HALF, layer:layer + 1]).then_inc(kept_ready[layer], 1)

            def pair(c0, n, first, last):
                for u in range(2):
                    c = c0 + u
                    start = first and u == 0
                    evacuate(1, c, layer1_group(c, CROSS_GROUPS), start)
                    if not (last and u == 1):
                        evacuate(0, c + 1, layer0_group(c + 1, FIRST_GROUPS), False)
                    evacuate(2, c, layer2_group(c, CROSS_GROUPS), start)

            act.wait_ge(bias_loaded, 16)
            evacuate(0, 0, layer0_group(0, FIRST_GROUPS), True)
            over_chunks(act, pair)
            act.wait_ge(top_loaded, 16 * TOP_DMAS)
            for t in range(tiles1):
                act.wait_ge(hid1_acc, t + 1)
                relu(hid1[:, t, :], mlp[t][:, 0:batch], top1_bias_sb[:, t:t + 1]).then_inc(hid1_ready, 1)
            for t in range(tiles2):
                act.wait_ge(hid2_acc, t + 1)
                relu(hid2[:, t, :], y[t][:, 0:batch], top2_bias_sb[:, t:t + 1]).then_inc(hid2_ready, 1)


_INS = ["ids", "offsets", "table", "w0a", "w0b", "w1", "w2", "biases", "dense",
        "top1", "top1_bias", "top2", "top2_bias", "top3"]


def _laid_out(inputs):
    import numpy as np

    f = {k: np.asarray(v) for k, v in inputs.items()}
    a = {}
    tables = [f[f"tbl_{i}"] for i in range(FIELDS)]
    starts = np.cumsum([0] + [t.shape[0] for t in tables[:-1]])
    batch = f["ids"].shape[0]
    chunks = batch // SAMPLES
    a["ids"] = f["ids"].T.reshape(FIELDS, chunks, SPLIT, LOOKUPS).transpose(0, 2, 1, 3).reshape(P, -1)
    a["offsets"] = np.repeat(starts.astype(np.int32), SPLIT * LOOKUPS).reshape(P, LOOKUPS)
    a["table"] = np.concatenate(tables, axis=0)
    w0 = f["L0_rec_W0"].reshape(P, FIELDS, FIELDS)
    d, g = np.meshgrid(np.arange(PAIR_TILES * SPLIT + SPLIT) % FIELDS, np.arange(FIELDS), indexing="ij")
    fwd = w0[:, g, (g + d) % FIELDS].reshape(P, PAIR_TILES + 1, P)
    rev = w0[:, (g + d) % FIELDS, g].reshape(P, PAIR_TILES + 1, P)
    a["w0a"] = fwd.transpose(2, 1, 0)
    a["w0b"] = rev.transpose(2, 1, 0)[:, :PAIR_TILES]
    for i in (1, 2):
        w = f[f"L0_rec_W{i}"].reshape(P, CROSS_TILES, P)
        a[f"w{i}"] = w.transpose(2, 1, 0)
    a["biases"] = np.stack([f[f"L0_rec_b{i}"] for i in range(3)], axis=1)
    a["dense"] = f["dense_ctx"].T
    a["top1"] = f["W_top1"]
    a["top1_bias"] = f["b_top1"].reshape(-1, P).T
    a["top2"] = f["W_top2"].reshape(-1, P, f["W_top2"].shape[1]).transpose(1, 0, 2)
    a["top2_bias"] = f["b_top2"].reshape(-1, P).T
    a["top3"] = f["W_top3"].reshape(-1, P).T
    return {k: np.ascontiguousarray(v) for k, v in a.items()}


def kernel(**inputs):
    import numpy as np
    import concourse.bacc as bacc
    from concourse.bass_utils import run_bass_kernel_spmd

    laid = _laid_out(inputs)
    batch = np.asarray(inputs["ids"]).shape[0]
    nc = bacc.Bacc("TRN2", target_bir_lowering=False, num_devices=1)
    args = [nc.dram_tensor(name, laid[name].shape, mybir.dt.from_np(laid[name].dtype),
                           kind="ExternalInput").ap() for name in _INS]
    out = nc.dram_tensor("score", (1, batch), F32, kind="ExternalOutput").ap()
    cin_tower(nc, *args, out)
    r = run_bass_kernel_spmd(nc, [{name: laid[name] for name in _INS}], core_ids=[0])
    return r.results[0]["score"].reshape(batch, 1)
```

```python
from contextlib import ExitStack

import concourse.bass as bass
from concourse import mybir

F32 = mybir.dt.float32
F32R = mybir.dt.float32r
I32 = mybir.dt.int32
ALU = mybir.AluOpType
ACT = mybir.ActivationFunctionType
AX_X = mybir.AxisListType.X

P = 128
FIELDS = 32
EMB = 16
HALF = 64
COLS = 512
SAMPLES = COLS // EMB
QUARTER = P // FIELDS
LOOKUPS = SAMPLES // QUARTER
PAIR_TILES = FIELDS // 2 // QUARTER
REST = 3 * FIELDS
CROSS_TILES = FIELDS * HALF // P
UNIT = 2
UNITS = CROSS_TILES // UNIT
UNITS0 = PAIR_TILES // UNIT

SPLIT = {1: "pool", 3: "pool", 5: "dve", 6: "dve"}
SPLITS = len(SPLIT)
PLAINS = UNITS - SPLITS
PLAIN_RING = 4
SPLIT_RING = 4
LAG = 2
LOW_LAG = 1
XREP_PARTS = 4
ROT_DMAS = 2 * QUARTER + REST // FIELDS
TOP_DMAS = 7
CHUNK_SPLITS = 2 * SPLITS
CHUNK_PLAINS = 2 * PLAINS + UNITS0
assert 2 * CHUNK_SPLITS % SPLIT_RING == 0 and 2 * CHUNK_PLAINS % PLAIN_RING == 0


def fixed(c, value):
    return isinstance(c, int) and c == value


def cin_tower(nc, ids, offsets, table, w0a, w0b, w0_rest, w1, w2, biases, dense,
              top1, top1_bias, top2, top2_bias, top3, out):
    chunks = ids.shape[1] // LOOKUPS
    batch = chunks * SAMPLES
    hidden1 = top1.shape[1]
    hidden2 = top2.shape[2]
    tiles1 = hidden1 // P
    tiles2 = hidden2 // P
    assert chunks % 2 == 0 and chunks >= 6 and batch <= COLS
    assert tiles1 <= 4 and tiles2 <= 2

    x0_dram = nc.dram_tensor("x0_rows", (chunks, 2 * FIELDS, COLS), F32, kind="Internal").ap()

    with ExitStack() as ctx:
        def sb(name, shape, dt=F32):
            return ctx.enter_context(nc.sbuf_tensor(name, shape, dt))

        def bank(name):
            return ctx.enter_context(nc.psum_tensor(name, [P, COLS], F32))

        def sem(name):
            return ctx.enter_context(nc.semaphore(name))

        idx_local = sb("idx_local", [P, chunks * LOOKUPS], I32)
        idx_offset = sb("idx_offset", [P, LOOKUPS], I32)
        idx = sb("idx", [P, 2, LOOKUPS], I32)
        gathered = sb("gathered", [P, 2, LOOKUPS * EMB])
        rot = sb("rot", [P, PAIR_TILES + 2, COLS])
        xrep = sb("xrep", [P, 2, CROSS_TILES, COLS])
        z_plain = sb("z_plain", [P, PLAIN_RING, UNIT, COLS])
        z_whole = sb("z_whole", [P, SPLIT_RING, UNIT, COLS])
        z_high = sb("z_high", [P, SPLIT_RING, UNIT, COLS], F32R)
        z_low = sb("z_low", [P, SPLIT_RING, UNIT, COLS], F32R)
        rest_whole = sb("rest_whole", [REST, COLS])
        rest_parts = sb("rest_parts", [REST, COLS], F32R)
        kept01 = sb("kept01", [P, 2, COLS])
        kept2 = sb("kept2", [P, COLS])
        w0_sb = sb("w0_sb", [P, PAIR_TILES, P])
        w0b_sb = sb("w0b_sb", [P, PAIR_TILES, P])
        w_sb = [None, sb("w1_sb", [P, CROSS_TILES, P]), sb("w2_sb", [P, CROSS_TILES, P])]
        w_high = [None] + [sb(f"w{i}_high", [P, SPLITS, UNIT, P], F32R) for i in (1, 2)]
        w_low = [None] + [sb(f"w{i}_low", [P, SPLITS, UNIT, P], F32R) for i in (1, 2)]
        w_rest = sb("w_rest", [REST, P])
        w_rest_parts = sb("w_rest_parts", [REST, P], F32R)
        bias_sb = sb("bias_sb", [P, 3])
        sums01 = sb("sums01", [P, batch])
        sums2 = sb("sums2", [P, batch])
        top1_bias_sb = sb("top1_bias_sb", [P, tiles1])
        top2_bias_sb = sb("top2_bias_sb", [P, tiles2])
        top3_sb = sb("top3_sb", [P, tiles2])
        out_sb = sb("out_sb", [1, batch])

        spare = z_whole[:].rearrange("p r u n -> p (r u n)")
        top1_sb = spare[:, 0:2 * hidden1].rearrange("p (t n) -> p t n", t=2)
        top1d_sb = spare[0:EMB, 2 * hidden1:3 * hidden1]
        top2_sb = spare[:, 3 * hidden1:3 * hidden1 + tiles1 * hidden2].rearrange("p (t n) -> p t n", t=tiles1)
        dense_at = 3 * hidden1 + tiles1 * hidden2
        dense_sb = spare[0:EMB, dense_at:dense_at + batch]
        assert dense_at + batch <= SPLIT_RING * UNIT * COLS
        hid1 = z_plain[:].rearrange("p r u n -> p (r u) n")[:, 0:tiles1, 0:batch]
        hid2 = z_plain[:].rearrange("p r u n -> p (r u) n")[:, tiles1:tiles1 + tiles2, 0:batch]

        y = [bank("y0"), bank("y1"), bank("y2")]
        h = [bank("h0"), bank("h1")]
        mlp = [bank(f"mlp{i}") for i in range(3)] + [h[0]]

        ids_loaded = sem("ids_loaded")
        w0_loaded = sem("w0_loaded")
        w_loaded = [None, sem("w1_loaded"), sem("w2_loaded")]
        bias_loaded = sem("bias_loaded")
        top_loaded = sem("top_loaded")
        idx_ready = sem("idx_ready")
        pool_steps = sem("pool_steps")
        rows_gathered = [sem("rows_gathered_a"), sem("rows_gathered_b")]
        x0_stored = [sem("x0_stored_a"), sem("x0_stored_b")]
        rot_loaded = sem("rot_loaded")
        xrep_loaded = [[sem(f"xrep_loaded_{'ab'[u]}{q}") for q in range(XREP_PARTS)] for u in range(2)]
        w0_folded = sem("w0_folded")
        w_high_ready = sem("w_high_ready")
        w_low_ready = sem("w_low_ready")
        plain_made = sem("plain_made")
        plain_used = sem("plain_used")
        whole_made = sem("whole_made")
        high_made = sem("high_made")
        low_made = {"dve": sem("low_made_dve"), "pool": sem("low_made_pool")}
        split_used = sem("split_used")
        rest_made = sem("rest_made")
        rest_high = sem("rest_high")
        rest_low = sem("rest_low")
        rest_used = sem("rest_used")
        h_ready = [sem("h0_ready"), sem("h1_ready")]
        kept_ready = [sem("kept0_ready"), sem("kept1_ready"), sem("kept2_ready")]
        kept01_summed = sem("kept01_summed")
        kept2_summed = sem("kept2_summed")
        hid1_acc = sem("hid1_acc")
        hid1_ready = sem("hid1_ready")
        hid2_acc = sem("hid2_acc")
        hid2_ready = sem("hid2_ready")
        score_acc = sem("score_acc")
        score_ready = sem("score_ready")
        out_stored = sem("out_stored")

        def plain0(c, k):
            return k if fixed(c, 0) else UNITS0 + CHUNK_PLAINS * (c - 1) + PLAINS + k

        def plain_number(layer, c, k):
            before = sum(1 for j in range(k) if j not in SPLIT)
            if layer == 2:
                before += PLAINS + (0 if fixed(c, chunks - 1) else UNITS0)
            return UNITS0 + CHUNK_PLAINS * c + before

        def split_number(layer, c, k):
            before = sum(1 for j in range(k) if j in SPLIT) + (SPLITS if layer == 2 else 0)
            return CHUNK_SPLITS * c + before

        def low_number(layer, c, k):
            same = [j for j in SPLIT if SPLIT[j] == SPLIT[k]]
            return 2 * len(same) * c + (len(same) if layer == 2 else 0) + sum(1 for j in same if j < k)

        def plain_slot(layer, u, c, k):
            at = k if layer == 0 and fixed(c, 0) else (
                plain0(u, k) if layer == 0 and u else
                plain0(2, k) if layer == 0 else plain_number(layer, c if fixed(c, chunks - 1) else u, k))
            return at % PLAIN_RING

        def split_slot(layer, u, k):
            return split_number(layer, u, k) % SPLIT_RING

        def over_chunks(eng, pair):
            pair(0, 1, True, False)
            with eng.Fori(1, chunks // 2 - 1) as i:
                pair(2 * i, i + 1, False, False)
            pair(chunks - 2, chunks // 2, False, True)

        block = ctx.enter_context(nc.Block())

        @block.sync
        def _(sp):
            sp.dma_start(idx_local[:], ids).then_inc(ids_loaded, 16)
            sp.dma_start(idx_offset[:], offsets).then_inc(ids_loaded, 16)
            sp.dma_start(w0_sb[:], w0a).then_inc(w0_loaded, 16)
            sp.dma_start(w0b_sb[:], w0b).then_inc(w0_loaded, 16)
            for part in range(3):
                sp.dma_start(w_rest[FIELDS * part:FIELDS * (part + 1), :], w0_rest).then_inc(w0_loaded, 16)
            sp.dma_start(bias_sb[:], biases).then_inc(bias_loaded, 16)
            sp.dma_start(w_sb[1][:], w1).then_inc(w_loaded[1], 16)
            sp.dma_start(w_sb[2][:], w2).then_inc(w_loaded[2], 16)

            def store_x0(c, u, n):
                sp.wait_ge(rows_gathered[u], 16 * LOOKUPS * n)
                rows = x0_dram[c].rearrange("(two f) (s n) -> two (f s) n", two=2, s=QUARTER)
                for copy in range(2):
                    sp.dma_start(rows[copy], gathered[:, u, :]).then_inc(x0_stored[u], 16)

            def load_rot(c, u, n, start):
                sp.wait_ge(x0_stored[u], 32 * n)
                if not start:
                    sp.wait_ge(rest_made, c)
                for k in range(QUARTER):
                    rows = slice(FIELDS * k, FIELDS * (k + 1))
                    sp.dma_start(rot[rows, 0, :], x0_dram[c][0:FIELDS, :]).then_inc(rot_loaded, 16)
                    win = x0_dram[c][k:k + FIELDS, :]
                    src = bass.AP(tensor=win.tensor, offset=win.offset,
                                  ap=[[COLS, FIELDS], [QUARTER * COLS, PAIR_TILES], [1, COLS]])
                    sp.dma_start(rot[rows, 1:1 + PAIR_TILES, :], src).then_inc(rot_loaded, 16)
                    if k < REST // FIELDS:
                        sp.dma_start(rot[rows, 1 + PAIR_TILES, :],
                                     x0_dram[c][FIELDS // 2:FIELDS // 2 + FIELDS, :]).then_inc(rot_loaded, 16)

            def load_xrep(c, u, n, first):
                if not first:
                    sp.wait_ge(plain_made, plain_number(2, c - 2, UNITS))
                    sp.wait_ge(whole_made, split_number(2, c - 2, UNITS))
                per = CROSS_TILES // XREP_PARTS
                for q in range(XREP_PARTS):
                    for half in range(2):
                        win = x0_dram[c][2 * per * q + half:2 * per * q + half + 1, :]
                        src = bass.AP(tensor=win.tensor, offset=win.offset,
                                      ap=[[0, HALF], [2 * COLS, per], [1, COLS]])
                        sp.dma_start(xrep[HALF * half:HALF * (half + 1), u, per * q:per * (q + 1), :],
                                     src).then_inc(xrep_loaded[u][q], 16)

            def pair(c, n, first, last):
                for u in range(2):
                    store_x0(c + u, u, n)
                    load_rot(c + u, u, n, first and u == 0)
                    load_xrep(c + u, u, n, first)

            over_chunks(sp, pair)
            sp.dma_start(top1_bias_sb[:], top1_bias).then_inc(top_loaded, 16)
            sp.dma_start(top2_bias_sb[:], top2_bias).then_inc(top_loaded, 16)
            sp.dma_start(top3_sb[:], top3).then_inc(top_loaded, 16)
            for who, s in low_made.items():
                sp.wait_ge(s, 2 * sum(1 for e in SPLIT.values() if e == who) * chunks)
            sp.dma_start(dense_sb, dense).then_inc(top_loaded, 16)
            sp.dma_start(top1_sb, top1[0:2 * P, :].rearrange("(t p) n -> p t n", t=2)).then_inc(top_loaded, 16)
            sp.dma_start(top1d_sb, top1[2 * P:2 * P + EMB, :]).then_inc(top_loaded, 16)
            sp.dma_start(top2_sb, top2).then_inc(top_loaded, 16)
            sp.wait_ge(score_ready, 1)
            sp.dma_start(out, out_sb[:]).then_inc(out_stored, 16)
            sp.wait_ge(out_stored, 16)

        def make_low(eng, ns, who, layer, c, u, k):
            slot = split_slot(layer, u, k)
            eng.wait_ge(high_made, split_number(layer, c, k) + 1)
            ns.tensor_tensor(out=z_low[:, slot, :, :], in0=z_whole[:, slot, :, :],
                             in1=z_high[:, slot, :, :].bitcast(F32),
                             op=ALU.subtract).then_inc(low_made[who], 1)

        @block.gpsimd
        def _(pool):
            def begin_gathers(c, u, n):
                if not fixed(n, 0):
                    pool.wait_ge(x0_stored[u], 32 * n)
                    pool.sem_inc(pool_steps, 1)
                pool.wait_ge(ids_loaded, 32)
                nc.gpsimd.tensor_tensor(out=idx[:, u, :],
                                        in0=idx_local[:, bass.ds(c * LOOKUPS, LOOKUPS)],
                                        in1=idx_offset[:], op=ALU.add).then_inc(idx_ready, 1)
                pool.wait_ge(idx_ready, c + 1)
                pool.sem_inc(pool_steps, 1)

            def gather(u, q):
                nc.gpsimd.indirect_dma_start(
                    out=gathered[:, u, q * EMB:(q + 1) * EMB], out_offset=None, in_=table,
                    in_offset=bass.IndirectOffsetOnAxis(ap=idx[:, u, q:q + 1], axis=0),
                ).then_inc(rows_gathered[u], 16)

            def pair(c0, n, first, last):
                for u in range(2):
                    c = c0 + u
                    if not last:
                        begin_gathers(c + 2, u, n)
                    for layer in (1, 2):
                        for k in [k for k in sorted(SPLIT) if SPLIT[k] == "pool"]:
                            make_low(pool, nc.gpsimd, "pool", layer, c, u, k)
                        if layer == 1 and not last:
                            for q in range(LOOKUPS):
                                gather(u, q)

            for u in range(2):
                begin_gathers(u, u, 0)
                for q in range(LOOKUPS):
                    gather(u, q)
            over_chunks(pool, pair)

        @block.vector
        def _(dve):
            dve.wait_ge(w0_loaded, 16 * 5)
            for lo, hi in ((FIELDS, HALF), (HALF, P)):
                nc.vector.tensor_tensor(out=w0_sb[lo:hi, 0, :], in0=w0_sb[lo:hi, 0, :],
                                        in1=w0b_sb[lo:hi, 0, :], op=ALU.add).then_inc(w0_folded, 1)
            nc.vector.tensor_tensor(out=w0_sb[:, 1:PAIR_TILES, :], in0=w0_sb[:, 1:PAIR_TILES, :],
                                    in1=w0b_sb[:, 1:, :], op=ALU.add).then_inc(w0_folded, 1)
            dve.wait_ge(w_high_ready, 1)
            nc.vector.tensor_tensor(out=w_rest_parts[2 * FIELDS:REST, :], in0=w_rest[2 * FIELDS:REST, :],
                                    in1=w_rest_parts[2 * FIELDS:REST, :].bitcast(F32),
                                    op=ALU.subtract).then_inc(w_low_ready, 1)
            for layer in (1, 2):
                for j, k in enumerate(sorted(SPLIT)):
                    dve.wait_ge(w_high_ready, 1 + (layer - 1) * SPLITS + j + 1)
                    nc.vector.tensor_tensor(out=w_low[layer][:, j, :, :],
                                            in0=w_sb[layer][:, UNIT * k:UNIT * (k + 1), :],
                                            in1=w_high[layer][:, j, :, :].bitcast(F32),
                                            op=ALU.subtract).then_inc(w_low_ready, 1)

            def make_layer0(c, u):
                dve.wait_ge(rot_loaded, 16 * ROT_DMAS * (c + 1))
                for k in range(UNITS0):
                    if not fixed(c, 0):
                        dve.wait_ge(plain_used, plain0(c, k) - PLAIN_RING + 1)
                    nc.vector.tensor_tensor(
                        out=z_plain[:, plain_slot(0, u, c, k), :, :],
                        in0=rot[:, 1 + UNIT * k:1 + UNIT * (k + 1), :],
                        in1=rot[:, 0:1, :].to_broadcast([P, UNIT, COLS]),
                        op=ALU.mult).then_inc(plain_made, 1)
                if not fixed(c, 0):
                    dve.wait_ge(rest_low, c)
                nc.vector.tensor_tensor(out=rest_whole[:], in0=rot[0:REST, 1 + PAIR_TILES, :],
                                        in1=rot[0:REST, 0, :], op=ALU.mult).then_inc(rest_made, 1)

            def make_rest_low(c):
                dve.wait_ge(rest_high, c + 1)
                rows = slice(FIELDS, 2 * FIELDS)
                nc.vector.tensor_tensor(out=rest_parts[rows, :], in0=rest_whole[rows, :],
                                        in1=rest_parts[rows, :].bitcast(F32),
                                        op=ALU.subtract).then_inc(rest_low, 1)

            def make_unit(layer, c, u, k, start):
                if k in SPLIT:
                    number = split_number(layer, c, k)
                    out, made = z_whole[:, split_slot(layer, u, k), :, :], whole_made
                    if not (start and number < SPLIT_RING):
                        l2, c2, k2 = earlier_split(layer, c, k)
                        dve.wait_ge(low_made[SPLIT[k2]], low_number(l2, c2, k2) + 1)
                else:
                    number = plain_number(layer, c, k)
                    out, made = z_plain[:, plain_slot(layer, u, c, k), :, :], plain_made
                    if not (start and number < PLAIN_RING):
                        dve.wait_ge(plain_used, number - PLAIN_RING + 1)
                nc.vector.tensor_tensor(
                    out=out, in0=xrep[:, u, UNIT * k:UNIT * (k + 1), :],
                    in1=h[layer - 1][:].unsqueeze(1).to_broadcast([P, UNIT, COLS]),
                    op=ALU.mult).then_inc(made, 1)

            def earlier_split(layer, c, k):
                order = [(layer_, k_) for layer_ in (1, 2) for k_ in sorted(SPLIT)]
                at = order.index((layer, k)) - SPLIT_RING
                back = 0
                while at < 0:
                    at += len(order)
                    back += 1
                return order[at][0], c - back, order[at][1]

            def sum_kept(c, u):
                cols = bass.ds(c * SAMPLES, SAMPLES)
                dve.wait_ge(kept_ready[0], c + 1)
                dve.wait_ge(kept_ready[1], c + 1)
                nc.vector.tensor_reduce(out=sums01[:, cols],
                                        in_=kept01[:, u, :].rearrange("p (s e) -> p s e", e=EMB),
                                        axis=AX_X, op=ALU.add).then_inc(kept01_summed, 1)
                dve.wait_ge(kept_ready[2], c + 1)
                nc.vector.tensor_reduce(out=sums2[:, cols], in_=kept2[:].rearrange("p (s e) -> p s e", e=EMB),
                                        axis=AX_X, op=ALU.add).then_inc(kept2_summed, 1)

            def make_layer(layer, c, u, n, start):
                dve.wait_ge(h_ready[layer - 1], 2 * (c + 1))
                due = []
                for k in range(UNITS):
                    if layer == 1 and k % (UNITS // XREP_PARTS) == 0:
                        q = k // (UNITS // XREP_PARTS)
                        dve.wait_ge(xrep_loaded[u][q], 32 * n)
                    make_unit(layer, c, u, k, start)
                    for j in [j for j in due if k - j >= LAG or k == UNITS - 1]:
                        make_low(dve, nc.vector, "dve", layer, c, u, j)
                        due.remove(j)
                    if SPLIT.get(k) == "dve":
                        due.append(k)
                assert not due

            def pair(c0, n, first, last):
                for u in range(2):
                    c = c0 + u
                    start = first and u == 0
                    end = last and u == 1
                    make_layer(1, c, u, n, start)
                    if not end:
                        make_layer0(c + 1, 1 - u)
                    if not start:
                        sum_kept(c - 1, 1 - u)
                    if not end:
                        make_rest_low(c + 1)
                    make_layer(2, c, u, n, False)

            make_layer0(0, 0)
            make_rest_low(0)
            over_chunks(dve, pair)
            sum_kept(chunks - 1, 1)
            dve.wait_ge(score_acc, 1)
            nc.vector.tensor_copy(out_sb[:], y[2][0:1, 0:batch]).then_inc(score_ready, 1)

        @block.tensor
        def _(pe):
            def layer0(c, u):
                if not fixed(c, 0):
                    pe.wait_ge(h_ready[0], 2 * c)
                    pe.wait_ge(kept_ready[0], c)
                for k in range(UNITS0):
                    pe.wait_ge(plain_made, plain0(c, k) + 1)
                    for t in range(UNIT):
                        last = nc.tensor.matmul(y[0][:], w0_sb[:, UNIT * k + t, :],
                                                z_plain[:, plain_slot(0, u, c, k), t, :],
                                                start=k + t == 0, stop=False)
                    last.then_inc(plain_used, 1)
                pe.wait_ge(rest_low, c + 1)
                nc.tensor.matmul(y[0][:], w_rest_parts[:], rest_parts[:],
                                 start=False, stop=True).then_inc(rest_used, 1)

            def low_product(layer, c, u, k):
                pe.wait_ge(low_made[SPLIT[k]], low_number(layer, c, k) + 1)
                slot = split_slot(layer, u, k)
                for t in range(UNIT):
                    last = nc.tensor.matmul(y[layer][:], w_high[layer][:, sorted(SPLIT).index(k), t, :],
                                            z_low[:, slot, t, :], start=False, stop=False)
                last.then_inc(split_used, 1)

            def cross(layer, c, u, start):
                if not start:
                    if layer == 1:
                        pe.wait_ge(h_ready[1], 2 * c)
                    pe.wait_ge(kept_ready[layer], c)
                due = []
                for k in range(UNITS):
                    if k in SPLIT:
                        pe.wait_ge(high_made, split_number(layer, c, k) + 1)
                        slot = split_slot(layer, u, k)
                        j = sorted(SPLIT).index(k)
                        for t in range(UNIT):
                            nc.tensor.matmul(y[layer][:], w_high[layer][:, j, t, :], z_high[:, slot, t, :],
                                             start=False, stop=False)
                            nc.tensor.matmul(y[layer][:], w_low[layer][:, j, t, :], z_high[:, slot, t, :],
                                             start=False, stop=False)
                    else:
                        pe.wait_ge(plain_made, plain_number(layer, c, k) + 1)
                        if k == UNITS - 1:
                            for j in due:
                                low_product(layer, c, u, j)
                            due = []
                        for t in range(UNIT):
                            last = nc.tensor.matmul(y[layer][:], w_sb[layer][:, UNIT * k + t, :],
                                                    z_plain[:, plain_slot(layer, u, c, k), t, :],
                                                    start=k + t == 0, stop=k == UNITS - 1 and t == UNIT - 1)
                        last.then_inc(plain_used, 1)
                    for j in [j for j in due if k - j >= LOW_LAG]:
                        low_product(layer, c, u, j)
                        due.remove(j)
                    if k in SPLIT:
                        due.append(k)

            def pair(c0, n, first, last):
                for u in range(2):
                    c = c0 + u
                    start = first and u == 0
                    cross(1, c, u, start)
                    if not (last and u == 1):
                        layer0(c + 1, 1 - u)
                    cross(2, c, u, start)

            pe.wait_ge(w0_folded, 3)
            pe.wait_ge(w_low_ready, 1)
            layer0(0, 0)
            pe.wait_ge(w_low_ready, 1 + 2 * SPLITS)
            over_chunks(pe, pair)

            pe.wait_ge(top_loaded, 16 * TOP_DMAS)
            pe.wait_ge(kept01_summed, chunks)
            pe.wait_ge(kept2_summed, chunks)
            for t in range(tiles1):
                cols = slice(P * t, P * (t + 1))
                nc.tensor.matmul(mlp[t][:, 0:batch], top1d_sb[:, cols], dense_sb, start=True, stop=False)
                nc.tensor.matmul(mlp[t][:, 0:batch], top1_sb[:, 0, cols], sums01[:], start=False, stop=False)
                nc.tensor.matmul(mlp[t][:, 0:batch], top1_sb[:, 1, cols], sums2[:],
                                 start=False, stop=True).then_inc(hid1_acc, 1)
            for t in range(tiles2):
                for k in range(tiles1):
                    pe.wait_ge(hid1_ready, k + 1)
                    last = nc.tensor.matmul(y[t][:, 0:batch], top2_sb[:, k, P * t:P * (t + 1)], hid1[:, k, :],
                                            start=k == 0, stop=k == tiles1 - 1)
                last.then_inc(hid2_acc, 1)
            for k in range(tiles2):
                pe.wait_ge(hid2_ready, k + 1)
                last = nc.tensor.matmul(y[2][0:1, 0:batch], top3_sb[:, k:k + 1], hid2[:, k, :],
                                        start=k == 0, stop=k == tiles2 - 1)
            last.then_inc(score_acc, 1)

        @block.scalar
        def _(act):
            def relu(dst, src, bias):
                return nc.scalar.activation(dst, src, ACT.Relu, bias=bias)

            def round_high(dst, src):
                return nc.scalar.activation(dst, src, ACT.Copy)

            def make_high(layer, c, u, k, start):
                act.wait_ge(whole_made, split_number(layer, c, k) + 1)
                if not (start and split_number(layer, c, k) < SPLIT_RING):
                    act.wait_ge(split_used, split_number(layer, c, k) - SPLIT_RING + 1)
                slot = split_slot(layer, u, k)
                round_high(z_high[:, slot, :, :], z_whole[:, slot, :, :]).then_inc(high_made, 1)

            def make_rest_high(c):
                act.wait_ge(rest_made, c + 1)
                if not fixed(c, 0):
                    act.wait_ge(rest_used, c)
                round_high(rest_parts[:], rest_whole[:]).then_inc(rest_high, 1)

            def evacuate(layer, c, u):
                if layer == 0:
                    act.wait_ge(rest_used, c + 1)
                else:
                    act.wait_ge(plain_used, plain_number(1, c, UNITS))
                up = slice(HALF, P)
                bias = bias_sb[up, layer:layer + 1]
                relu(h[layer][up, :], y[layer][up, :], bias).then_inc(h_ready[layer], 1)
                relu(h[layer][0:HALF, :], y[layer][up, :], bias).then_inc(h_ready[layer], 1)
                if layer == 0 and not (fixed(c, 0) or fixed(c, 1)):
                    act.wait_ge(kept01_summed, c - 1)
                relu(kept01[HALF * layer:HALF * (layer + 1), u, :], y[layer][0:HALF, :],
                     bias_sb[0:HALF, layer:layer + 1]).then_inc(kept_ready[layer], 1)

            def evacuate2(c):
                act.wait_ge(plain_used, plain_number(2, c, UNITS))
                if not fixed(c, 0):
                    act.wait_ge(kept2_summed, c)
                relu(kept2[:], y[2][:], bias_sb[:, 2:3]).then_inc(kept_ready[2], 1)

            def pair(c0, n, first, last):
                for u in range(2):
                    c = c0 + u
                    start = first and u == 0
                    end = last and u == 1
                    for j, k in enumerate(sorted(SPLIT)):
                        make_high(1, c, u, k, start)
                        if j == 1 and not start:
                            evacuate2(c - 1)
                    if not end:
                        make_rest_high(c + 1)
                    evacuate(1, c, u)
                    for j, k in enumerate(sorted(SPLIT)):
                        make_high(2, c, u, k, False)
                        if j == 1 and not end:
                            evacuate(0, c + 1, 1 - u)

            act.wait_ge(w0_loaded, 16 * 5)
            round_high(w_rest_parts[:], w_rest[:]).then_inc(w_high_ready, 1)
            for layer in (1, 2):
                act.wait_ge(w_loaded[layer], 16)
                for j, k in enumerate(sorted(SPLIT)):
                    round_high(w_high[layer][:, j, :, :],
                               w_sb[layer][:, UNIT * k:UNIT * (k + 1), :]).then_inc(w_high_ready, 1)
            act.wait_ge(bias_loaded, 16)
            make_rest_high(0)
            evacuate(0, 0, 0)
            over_chunks(act, pair)
            evacuate2(chunks - 1)
            act.wait_ge(top_loaded, 16 * TOP_DMAS)
            for t in range(tiles1):
                act.wait_ge(hid1_acc, t + 1)
                relu(hid1[:, t, :], mlp[t][:, 0:batch], top1_bias_sb[:, t:t + 1]).then_inc(hid1_ready, 1)
            for t in range(tiles2):
                act.wait_ge(hid2_acc, t + 1)
                relu(hid2[:, t, :], y[t][:, 0:batch], top2_bias_sb[:, t:t + 1]).then_inc(hid2_ready, 1)


_INS = ["ids", "offsets", "table", "w0a", "w0b", "w0_rest", "w1", "w2", "biases", "dense",
        "top1", "top1_bias", "top2", "top2_bias", "top3"]


def _laid_out(inputs):
    import numpy as np

    f = {k: np.asarray(v) for k, v in inputs.items()}
    a = {}
    tables = [f[f"tbl_{i}"] for i in range(FIELDS)]
    starts = np.cumsum([0] + [t.shape[0] for t in tables[:-1]])
    batch = f["ids"].shape[0]
    chunks = batch // SAMPLES
    a["ids"] = f["ids"].T.reshape(FIELDS, chunks, QUARTER, LOOKUPS).transpose(0, 2, 1, 3).reshape(P, -1)
    a["offsets"] = np.repeat(starts.astype(np.int32), QUARTER * LOOKUPS).reshape(P, LOOKUPS)
    a["table"] = np.concatenate(tables, axis=0)
    w0 = f["L0_rec_W0"].reshape(P, FIELDS, FIELDS)
    d, g = np.meshgrid(np.arange(FIELDS // 2), np.arange(FIELDS), indexing="ij")
    for name, rows, cols in (("w0a", g, (g + d) % FIELDS), ("w0b", (g + d) % FIELDS, g)):
        a[name] = w0[:, rows, cols].reshape(P, PAIR_TILES, P).transpose(2, 1, 0)
    g = np.arange(FIELDS)
    a["w0_rest"] = w0[:, g, (g + FIELDS // 2) % FIELDS].T
    for i in (1, 2):
        w = f[f"L0_rec_W{i}"].reshape(P, CROSS_TILES, P)
        a[f"w{i}"] = w.transpose(2, 1, 0)
    a["biases"] = np.stack([f[f"L0_rec_b{i}"] for i in range(3)], axis=1)
    a["dense"] = f["dense_ctx"].T
    a["top1"] = f["W_top1"]
    a["top1_bias"] = f["b_top1"].reshape(-1, P).T
    a["top2"] = f["W_top2"].reshape(-1, P, f["W_top2"].shape[1]).transpose(1, 0, 2)
    a["top2_bias"] = f["b_top2"].reshape(-1, P).T
    a["top3"] = f["W_top3"].reshape(-1, P).T
    return {k: np.ascontiguousarray(v) for k, v in a.items()}


def kernel(**inputs):
    import numpy as np
    import concourse.bacc as bacc
    from concourse.bass_utils import run_bass_kernel_spmd

    laid = _laid_out(inputs)
    batch = np.asarray(inputs["ids"]).shape[0]
    nc = bacc.Bacc("TRN2", target_bir_lowering=False, num_devices=1)
    args = [nc.dram_tensor(name, laid[name].shape, mybir.dt.from_np(laid[name].dtype),
                           kind="ExternalInput").ap() for name in _INS]
    out = nc.dram_tensor("score", (1, batch), F32, kind="ExternalOutput").ap()
    cin_tower(nc, *args, out)
    r = run_bass_kernel_spmd(nc, [{name: laid[name] for name in _INS}], core_ids=[0])
    return r.results[0]["score"].reshape(batch, 1)
```

```python
from contextlib import ExitStack

import concourse.bass as bass
from concourse import mybir

F32 = mybir.dt.float32
F32R = mybir.dt.float32r
I32 = mybir.dt.int32
ALU = mybir.AluOpType
ACT = mybir.ActivationFunctionType
AX_X = mybir.AxisListType.X

P = 128
FIELDS = 32
EMB = 16
HALF = 64
COLS = 512
SAMPLES = COLS // EMB
QUARTER = P // FIELDS
LOOKUPS = SAMPLES // QUARTER
PAIR_TILES = FIELDS // 2 // QUARTER
ROWS = FIELDS + FIELDS // 2
REST = 3 * FIELDS
CROSS_TILES = FIELDS * HALF // P
UNIT = 2
UNITS = CROSS_TILES // UNIT
UNITS0 = PAIR_TILES // UNIT

SPLIT = {1: "pool", 2: "pool", 4: "dve", 5: "pool", 6: "dve"}
SPLITS = len(SPLIT)
PLAINS = UNITS - SPLITS
PLAIN_RING = 4
SPLIT_RING = 5
LAG = 2
LOW_LAG = 3
XREP_PARTS = 2
TOP_DMAS = 5
EARLY_TOPS = 3
GATHERS_BEFORE_REST = 4
CHUNK_SPLITS = 2 * SPLITS
CHUNK_PLAINS = 2 * PLAINS + UNITS0
assert 2 * CHUNK_SPLITS % SPLIT_RING == 0 and 2 * CHUNK_PLAINS % PLAIN_RING == 0


def fixed(c, value):
    return isinstance(c, int) and c == value


def cin_tower(nc, ids, table, w0a, w0b, w0_rest, w1, w2, biases, dense,
              top1, top1_bias, top2, top2_bias, top3, out):
    chunks = ids.shape[1] // LOOKUPS - 1
    batch = chunks * SAMPLES
    hidden1 = top1.shape[1]
    hidden2 = top2.shape[2]
    tiles1 = hidden1 // P
    tiles2 = hidden2 // P
    assert chunks % 2 == 0 and chunks >= 6 and batch <= COLS
    assert tiles1 == EARLY_TOPS + 1 and tiles2 <= 2

    x0_dram = nc.dram_tensor("x0_rows", (chunks, ROWS, COLS), F32, kind="Internal").ap()

    with ExitStack() as ctx:
        def sb(name, shape, dt=F32):
            return ctx.enter_context(nc.sbuf_tensor(name, shape, dt))

        def bank(name):
            return ctx.enter_context(nc.psum_tensor(name, [P, COLS], F32))

        def sem(name):
            return ctx.enter_context(nc.semaphore(name))

        idx_local = sb("idx_local", [P, (chunks + 1) * LOOKUPS], I32)
        idx_offset = idx_local[:, chunks * LOOKUPS:(chunks + 1) * LOOKUPS]
        idx = sb("idx", [P, 2, LOOKUPS], I32)
        gathered = sb("gathered", [P, 2, LOOKUPS * EMB])
        rot = sb("rot", [P, PAIR_TILES + 1, COLS])
        rest_rot = sb("rest_rot", [FIELDS, 2, COLS])
        xrep = sb("xrep", [P, 2, CROSS_TILES, COLS])
        z_plain = sb("z_plain", [P, PLAIN_RING, UNIT, COLS])
        z_whole = sb("z_whole", [P, SPLIT_RING, UNIT, COLS])
        z_high = sb("z_high", [P, SPLIT_RING, UNIT, COLS], F32R)
        z_low = sb("z_low", [P, SPLIT_RING, UNIT, COLS], F32R)
        rest_whole = sb("rest_whole", [FIELDS, COLS])
        rest_parts = sb("rest_parts", [REST, COLS], F32R)
        kept01 = sb("kept01", [P, 2, COLS])
        kept2 = sb("kept2", [P, COLS])
        w0_sb = sb("w0_sb", [P, PAIR_TILES, P])
        w0b_sb = sb("w0b_sb", [P, PAIR_TILES, P])
        w_plain = [None] + [sb(f"w{i}_plain", [P, PLAINS, UNIT, P]) for i in (1, 2)]
        w_low = [None] + [sb(f"w{i}_low", [P, SPLITS, UNIT, P], F32R) for i in (1, 2)]
        w_high = [None] + [sb(f"w{i}_high", [P, SPLITS, UNIT, P], F32R) for i in (1, 2)]
        w_rest = sb("w_rest", [REST, P])
        w_rest_parts = sb("w_rest_parts", [REST, P], F32R)
        bias_sb = sb("bias_sb", [P, 3])
        sums01 = sb("sums01", [P, batch])
        sums2 = sb("sums2", [P, batch])
        top1_bias_sb = sb("top1_bias_sb", [P, tiles1])
        top2_bias_sb = sb("top2_bias_sb", [P, tiles2])
        top3_sb = sb("top3_sb", [P, tiles2])
        out_sb = sb("out_sb", [1, batch])

        dense_sb = sb("dense_sb", [EMB, batch])
        top1d_sb = sb("top1d_sb", [EMB, hidden1])

        staging = z_whole[:].rearrange("p r u n -> p (r u n)")[:, 0:2 * SPLITS * UNIT * P]
        staging = staging.rearrange("p (l j t n) -> p l j t n", l=2, j=SPLITS, t=UNIT)
        w_whole = [None, staging[:, 0], staging[:, 1]]

        spare = xrep[:, 0, :, :].rearrange("p j n -> p (j n)")
        top1_sb = spare[:, 0:2 * hidden1].rearrange("p (t n) -> p t n", t=2)
        top2_sb = spare[:, 2 * hidden1:2 * hidden1 + tiles1 * hidden2].rearrange("p (t n) -> p t n", t=tiles1)
        hid1 = z_plain[:].rearrange("p r u n -> p (r u) n")[:, 0:tiles1, 0:batch]
        hid2 = z_plain[:].rearrange("p r u n -> p (r u) n")[:, tiles1:tiles1 + tiles2, 0:batch]

        y = [bank("y0"), bank("y1"), bank("y2")]
        h = [bank("h0"), bank("h1")]
        mlp = [bank(f"mlp{i}") for i in range(EARLY_TOPS)] + [h[0]]

        ids_loaded = sem("ids_loaded")
        w0_loaded = sem("w0_loaded")
        w_loaded = [None, sem("w1_loaded"), sem("w2_loaded")]
        bias_loaded = sem("bias_loaded")
        dense_loaded = sem("dense_loaded")
        top_loaded = sem("top_loaded")
        idx_ready = sem("idx_ready")
        pool_steps = sem("pool_steps")
        rows_gathered = [sem("rows_gathered_a"), sem("rows_gathered_b")]
        x0_stored = [sem("x0_stored_a"), sem("x0_stored_b")]
        rest_loaded = sem("rest_loaded")
        rot_loaded = [sem(f"rot_loaded{k}") for k in range(UNITS0)]
        xrep_loaded = [[sem(f"xrep_loaded_{'ab'[u]}{q}") for q in range(XREP_PARTS)] for u in range(2)]
        w0_folded = sem("w0_folded")
        w_high_ready = sem("w_high_ready")
        w_low_ready = sem("w_low_ready")
        plain_made = sem("plain_made")
        plain_used = sem("plain_used")
        whole_made = sem("whole_made")
        high_made = sem("high_made")
        low_made = {"dve": sem("low_made_dve"), "pool": sem("low_made_pool")}
        split_used = sem("split_used")
        rest_made = sem("rest_made")
        rest_high = sem("rest_high")
        rest_low = sem("rest_low")
        rest_used = sem("rest_used")
        h_ready = [sem("h0_ready"), sem("h1_ready")]
        kept_ready = [sem("kept0_ready"), sem("kept1_ready"), sem("kept2_ready")]
        kept01_summed = sem("kept01_summed")
        kept2_summed = sem("kept2_summed")
        hid1_acc = sem("hid1_acc")
        hid1_ready = sem("hid1_ready")
        hid2_acc = sem("hid2_acc")
        hid2_ready = sem("hid2_ready")
        score_acc = sem("score_acc")
        score_ready = sem("score_ready")
        out_stored = sem("out_stored")

        def plain0(c, k):
            return k if fixed(c, 0) else UNITS0 + CHUNK_PLAINS * (c - 1) + PLAINS + k

        def plains_before(k):
            return sum(1 for j in range(k) if j not in SPLIT)

        def plain_number(layer, c, k):
            before = plains_before(k)
            if layer == 2:
                before += PLAINS + (0 if fixed(c, chunks - 1) else UNITS0)
            return UNITS0 + CHUNK_PLAINS * c + before

        def split_number(layer, c, k):
            before = sum(1 for j in range(k) if j in SPLIT) + (SPLITS if layer == 2 else 0)
            return CHUNK_SPLITS * c + before

        def low_number(layer, c, k):
            same = [j for j in sorted(SPLIT) if SPLIT[j] == SPLIT[k]]
            return 2 * len(same) * c + (len(same) if layer == 2 else 0) + same.index(k)

        def plain_slot(layer, u, c, k):
            at = k if layer == 0 and fixed(c, 0) else (
                plain0(u, k) if layer == 0 and u else
                plain0(2, k) if layer == 0 else plain_number(layer, c if fixed(c, chunks - 1) else u, k))
            return at % PLAIN_RING

        def split_slot(layer, u, k):
            return split_number(layer, u, k) % SPLIT_RING

        def over_chunks(eng, pair):
            pair(0, 1, True, False)
            with eng.Fori(1, chunks // 2 - 1) as i:
                pair(2 * i, i + 1, False, False)
            pair(chunks - 2, chunks // 2, False, True)

        block = ctx.enter_context(nc.Block())

        @block.sync
        def _(sp):
            sp.dma_start(idx_local[:], ids).then_inc(ids_loaded, 16)
            sp.dma_start(w0_sb[:], w0a).then_inc(w0_loaded, 16)
            sp.dma_start(w0b_sb[:], w0b).then_inc(w0_loaded, 16)
            for part in range(3):
                sp.dma_start(w_rest[FIELDS * part:FIELDS * (part + 1), :], w0_rest).then_inc(w0_loaded, 16)
            sp.dma_start(bias_sb[:], biases).then_inc(bias_loaded, 16)
            for layer, w in ((1, w1), (2, w2)):
                sp.dma_start(w_whole[layer], w[:, PLAINS:UNITS]).then_inc(w_loaded[layer], 16)
                sp.dma_start(w_plain[layer][:], w[:, 0:PLAINS]).then_inc(w_loaded[layer], 16)
            sp.dma_start(dense_sb[:], dense).then_inc(dense_loaded, 16)
            sp.dma_start(top1d_sb[:], top1[2 * P:2 * P + EMB, :]).then_inc(dense_loaded, 16)

            def store_x0(c, u, n):
                sp.wait_ge(rows_gathered[u], 16 * LOOKUPS * n)
                rows = x0_dram[c].rearrange("f (s n) -> (f s) n", s=QUARTER)
                sp.dma_start(rows[0:P, :], gathered[:, u, :]).then_inc(x0_stored[u], 16)
                sp.dma_start(rows[P:ROWS * QUARTER, :], gathered[0:P // 2, u, :]).then_inc(x0_stored[u], 16)

            def load_rot(c, u, n, start):
                sp.wait_ge(x0_stored[u], 32 * n)
                if not start:
                    sp.wait_ge(rest_made, c)
                    sp.wait_ge(plain_made, plain0(c - 1, UNITS0))
                at = x0_dram[c]

                def window(first_row, *dims):
                    return bass.AP(tensor=at.tensor, offset=at[first_row:first_row + 1, :].offset,
                                   ap=[[COLS * step, count] for step, count in dims] + [[1, COLS]])

                sp.dma_start(rest_rot[:], window(0, (1, FIELDS), (FIELDS // 2, 2))).then_inc(rest_loaded, 16)
                sp.dma_start(rot[:, 0, :], window(0, (1, FIELDS), (0, QUARTER))).then_inc(rot_loaded[0], 16)
                for k in range(UNITS0):
                    sp.dma_start(rot[:, 1 + UNIT * k:1 + UNIT * (k + 1), :],
                                 window(UNIT * k, (1, FIELDS), (PAIR_TILES, QUARTER), (1, UNIT))
                                 ).then_inc(rot_loaded[k], 16)

            def load_xrep(c, u, n, first):
                if not first:
                    sp.wait_ge(plain_made, plain_number(2, c - 2, UNITS))
                    sp.wait_ge(whole_made, split_number(2, c - 2, UNITS))
                per = CROSS_TILES // XREP_PARTS
                for q in range(XREP_PARTS):
                    for half in range(2):
                        win = x0_dram[c][2 * per * q + half:2 * per * q + half + 1, :]
                        src = bass.AP(tensor=win.tensor, offset=win.offset,
                                      ap=[[0, HALF], [2 * COLS, per], [1, COLS]])
                        sp.dma_start(xrep[HALF * half:HALF * (half + 1), u, per * q:per * (q + 1), :],
                                     src).then_inc(xrep_loaded[u][q], 16)

            def pair(c, n, first, last):
                for u in range(2):
                    store_x0(c + u, u, n)
                    load_rot(c + u, u, n, first and u == 0)
                    load_xrep(c + u, u, n, first)

            over_chunks(sp, pair)
            sp.dma_start(top1_bias_sb[:], top1_bias).then_inc(top_loaded, 16)
            sp.dma_start(top2_bias_sb[:], top2_bias).then_inc(top_loaded, 16)
            sp.dma_start(top3_sb[:], top3).then_inc(top_loaded, 16)
            sp.wait_ge(plain_made, plain_number(2, chunks - 2, UNITS))
            sp.wait_ge(whole_made, split_number(2, chunks - 2, UNITS))
            sp.dma_start(top1_sb, top1[0:2 * P, :].rearrange("(t p) n -> p t n", t=2)).then_inc(top_loaded, 16)
            sp.dma_start(top2_sb, top2).then_inc(top_loaded, 16)
            sp.wait_ge(score_ready, 1)
            sp.dma_start(out, out_sb[:]).then_inc(out_stored, 16)
            sp.wait_ge(out_stored, 16)

        def make_low(eng, ns, who, layer, c, u, k):
            slot = split_slot(layer, u, k)
            eng.wait_ge(high_made, split_number(layer, c, k) + 1)
            ns.tensor_tensor(out=z_low[:, slot, :, :], in0=z_whole[:, slot, :, :],
                             in1=z_high[:, slot, :, :].bitcast(F32),
                             op=ALU.subtract).then_inc(low_made[who], 1)

        @block.gpsimd
        def _(pool):
            def make_rest_low(c):
                pool.wait_ge(rest_high, 3 * c + 1)
                nc.gpsimd.tensor_tensor(out=rest_parts[0:FIELDS, :], in0=rest_whole[:],
                                        in1=rest_parts[0:FIELDS, :].bitcast(F32),
                                        op=ALU.subtract).then_inc(rest_low, 1)

            def begin_gathers(c, u, n):
                if not fixed(n, 0):
                    pool.wait_ge(x0_stored[u], 32 * n)
                    pool.sem_inc(pool_steps, 1)
                pool.wait_ge(ids_loaded, 16)
                nc.gpsimd.tensor_tensor(out=idx[:, u, :],
                                        in0=idx_local[:, bass.ds(c * LOOKUPS, LOOKUPS)],
                                        in1=idx_offset, op=ALU.add).then_inc(idx_ready, 1)
                pool.wait_ge(idx_ready, c + 1)
                pool.sem_inc(pool_steps, 1)

            def gather(u, q):
                nc.gpsimd.indirect_dma_start(
                    out=gathered[:, u, q * EMB:(q + 1) * EMB], out_offset=None, in_=table,
                    in_offset=bass.IndirectOffsetOnAxis(ap=idx[:, u, q:q + 1], axis=0),
                ).then_inc(rows_gathered[u], 16)

            def pair(c0, n, first, last):
                for u in range(2):
                    c = c0 + u
                    if not last:
                        begin_gathers(c + 2, u, n)
                    for k in sorted(SPLIT):
                        if SPLIT[k] == "pool":
                            make_low(pool, nc.gpsimd, "pool", 1, c, u, k)
                    if not last:
                        for q in range(GATHERS_BEFORE_REST):
                            gather(u, q)
                    if not (last and u == 1):
                        make_rest_low(c + 1)
                    if not last:
                        for q in range(GATHERS_BEFORE_REST, LOOKUPS):
                            gather(u, q)
                    for k in sorted(SPLIT):
                        if SPLIT[k] == "pool":
                            make_low(pool, nc.gpsimd, "pool", 2, c, u, k)

            for u in range(2):
                begin_gathers(u, u, 0)
                for q in range(LOOKUPS):
                    gather(u, q)
            make_rest_low(0)
            over_chunks(pool, pair)

        @block.vector
        def _(dve):
            dve.wait_ge(w0_loaded, 16 * 5)
            nc.vector.tensor_tensor(out=w0_sb[:], in0=w0_sb[:], in1=w0b_sb[:], op=ALU.add).then_inc(w0_folded, 1)
            dve.wait_ge(w_high_ready, 1)
            nc.vector.tensor_tensor(out=w_rest_parts[2 * FIELDS:REST, :], in0=w_rest[2 * FIELDS:REST, :],
                                    in1=w_rest_parts[2 * FIELDS:REST, :].bitcast(F32),
                                    op=ALU.subtract).then_inc(w_low_ready, 1)
            for layer in (1, 2):
                for j, k in enumerate(sorted(SPLIT)):
                    dve.wait_ge(w_high_ready, 1 + (layer - 1) * SPLITS + j + 1)
                    nc.vector.tensor_tensor(out=w_low[layer][:, j, :, :],
                                            in0=w_whole[layer][:, j, :, :],
                                            in1=w_high[layer][:, j, :, :].bitcast(F32),
                                            op=ALU.subtract).then_inc(w_low_ready, 1)

            def make_layer0(c, u):
                dve.wait_ge(rest_loaded, 16 * (c + 1))
                if not fixed(c, 0):
                    dve.wait_ge(rest_low, c)
                    dve.wait_ge(rest_high, 3 * c)
                nc.vector.tensor_tensor(out=rest_whole[:], in0=rest_rot[:, 1, :],
                                        in1=rest_rot[:, 0, :], op=ALU.mult).then_inc(rest_made, 1)
                for k in range(UNITS0):
                    dve.wait_ge(rot_loaded[k], (32 if k == 0 else 16) * (c + 1))
                    if not fixed(c, 0):
                        dve.wait_ge(plain_used, plain0(c, k) - PLAIN_RING + 1)
                    nc.vector.tensor_tensor(
                        out=z_plain[:, plain_slot(0, u, c, k), :, :],
                        in0=rot[:, 1 + UNIT * k:1 + UNIT * (k + 1), :],
                        in1=rot[:, 0:1, :].to_broadcast([P, UNIT, COLS]),
                        op=ALU.mult).then_inc(plain_made, 1)

            def make_unit(layer, c, u, k, start):
                if k in SPLIT:
                    number = split_number(layer, c, k)
                    out, made = z_whole[:, split_slot(layer, u, k), :, :], whole_made
                    if not (start and number < SPLIT_RING):
                        l2, c2, k2 = earlier_split(layer, c, k)
                        dve.wait_ge(low_made[SPLIT[k2]], low_number(l2, c2, k2) + 1)
                else:
                    number = plain_number(layer, c, k)
                    out, made = z_plain[:, plain_slot(layer, u, c, k), :, :], plain_made
                    if not (start and number < PLAIN_RING):
                        dve.wait_ge(plain_used, number - PLAIN_RING + 1)
                nc.vector.tensor_tensor(
                    out=out, in0=xrep[:, u, UNIT * k:UNIT * (k + 1), :],
                    in1=h[layer - 1][:].unsqueeze(1).to_broadcast([P, UNIT, COLS]),
                    op=ALU.mult).then_inc(made, 1)

            def earlier_split(layer, c, k):
                order = [(layer_, k_) for layer_ in (1, 2) for k_ in sorted(SPLIT)]
                at = order.index((layer, k)) - SPLIT_RING
                back = 0
                while at < 0:
                    at += len(order)
                    back += 1
                return order[at][0], c - back, order[at][1]

            def sum_kept(c, u):
                cols = bass.ds(c * SAMPLES, SAMPLES)
                dve.wait_ge(kept_ready[0], c + 1)
                dve.wait_ge(kept_ready[1], c + 1)
                nc.vector.tensor_reduce(out=sums01[:, cols],
                                        in_=kept01[:, u, :].rearrange("p (s e) -> p s e", e=EMB),
                                        axis=AX_X, op=ALU.add).then_inc(kept01_summed, 1)
                dve.wait_ge(kept_ready[2], c + 1)
                nc.vector.tensor_reduce(out=sums2[:, cols], in_=kept2[:].rearrange("p (s e) -> p s e", e=EMB),
                                        axis=AX_X, op=ALU.add).then_inc(kept2_summed, 1)

            def make_layer(layer, c, u, n, start):
                dve.wait_ge(h_ready[layer - 1], 2 * (c + 1))
                due = []
                for k in range(UNITS):
                    if layer == 1 and k % (UNITS // XREP_PARTS) == 0:
                        q = k // (UNITS // XREP_PARTS)
                        dve.wait_ge(xrep_loaded[u][q], 32 * n)
                    make_unit(layer, c, u, k, start)
                    for j in [j for j in due if k - j >= LAG or k == UNITS - 1]:
                        make_low(dve, nc.vector, "dve", layer, c, u, j)
                        due.remove(j)
                    if SPLIT.get(k) == "dve":
                        due.append(k)
                assert not due

            def pair(c0, n, first, last):
                for u in range(2):
                    c = c0 + u
                    start = first and u == 0
                    end = last and u == 1
                    make_layer(1, c, u, n, start)
                    if not end:
                        make_layer0(c + 1, 1 - u)
                    if not start:
                        sum_kept(c - 1, 1 - u)
                    make_layer(2, c, u, n, False)

            make_layer0(0, 0)
            over_chunks(dve, pair)
            sum_kept(chunks - 1, 1)
            dve.wait_ge(score_acc, 1)
            nc.vector.tensor_copy(out_sb[:], y[2][0:1, 0:batch]).then_inc(score_ready, 1)

        @block.tensor
        def _(pe):
            def layer0(c, u):
                if not fixed(c, 0):
                    pe.wait_ge(h_ready[0], 2 * c)
                    pe.wait_ge(kept_ready[0], c)
                for k in range(UNITS0):
                    pe.wait_ge(plain_made, plain0(c, k) + 1)
                    for t in range(UNIT):
                        last = nc.tensor.matmul(y[0][:], w0_sb[:, UNIT * k + t, :],
                                                z_plain[:, plain_slot(0, u, c, k), t, :],
                                                start=k + t == 0, stop=False)
                    last.then_inc(plain_used, 1)
                pe.wait_ge(rest_low, c + 1)
                pe.wait_ge(rest_high, 3 * (c + 1))
                nc.tensor.matmul(y[0][:], w_rest_parts[:], rest_parts[:],
                                 start=False, stop=True).then_inc(rest_used, 1)

            def low_product(layer, c, u, k):
                pe.wait_ge(low_made[SPLIT[k]], low_number(layer, c, k) + 1)
                slot = split_slot(layer, u, k)
                for t in range(UNIT):
                    last = nc.tensor.matmul(y[layer][:], w_high[layer][:, sorted(SPLIT).index(k), t, :],
                                            z_low[:, slot, t, :], start=False, stop=False)
                last.then_inc(split_used, 1)

            def cross(layer, c, u, start):
                if not start:
                    if layer == 1:
                        pe.wait_ge(h_ready[1], 2 * c)
                    pe.wait_ge(kept_ready[layer], c)
                due = []
                for k in range(UNITS):
                    if k in SPLIT:
                        pe.wait_ge(high_made, split_number(layer, c, k) + 1)
                        slot = split_slot(layer, u, k)
                        j = sorted(SPLIT).index(k)
                        for t in range(UNIT):
                            nc.tensor.matmul(y[layer][:], w_high[layer][:, j, t, :], z_high[:, slot, t, :],
                                             start=False, stop=False)
                            nc.tensor.matmul(y[layer][:], w_low[layer][:, j, t, :], z_high[:, slot, t, :],
                                             start=False, stop=False)
                    else:
                        pe.wait_ge(plain_made, plain_number(layer, c, k) + 1)
                        if k == UNITS - 1:
                            for j in due:
                                low_product(layer, c, u, j)
                            due = []
                        for t in range(UNIT):
                            last = nc.tensor.matmul(y[layer][:], w_plain[layer][:, plains_before(k), t, :],
                                                    z_plain[:, plain_slot(layer, u, c, k), t, :],
                                                    start=k + t == 0, stop=k == UNITS - 1 and t == UNIT - 1)
                        last.then_inc(plain_used, 1)
                    for j in [j for j in due if k - j >= LOW_LAG]:
                        low_product(layer, c, u, j)
                        due.remove(j)
                    if k in SPLIT:
                        due.append(k)

            def pair(c0, n, first, last):
                for u in range(2):
                    c = c0 + u
                    start = first and u == 0
                    cross(1, c, u, start)
                    if not (last and u == 1):
                        layer0(c + 1, 1 - u)
                    if last and u == 1:
                        top_first(slice(0, batch - SAMPLES), chunks - 1)
                    cross(2, c, u, start)

            def top_dense(t):
                nc.tensor.matmul(mlp[t][:, 0:batch], top1d_sb[:, P * t:P * (t + 1)], dense_sb[:],
                                 start=True, stop=False)

            def top_first(cols, summed):
                pe.wait_ge(top_loaded, 16 * TOP_DMAS)
                pe.wait_ge(kept01_summed, summed)
                for t in range(tiles1):
                    if t >= EARLY_TOPS and summed < chunks:
                        top_dense(t)
                    nc.tensor.matmul(mlp[t][:, cols], top1_sb[:, 0, P * t:P * (t + 1)], sums01[:, cols],
                                     start=False, stop=False)

            pe.wait_ge(dense_loaded, 32)
            for t in range(EARLY_TOPS):
                top_dense(t)
            pe.wait_ge(w0_folded, 1)
            pe.wait_ge(w_low_ready, 1)
            layer0(0, 0)
            pe.wait_ge(w_low_ready, 1 + 2 * SPLITS)
            over_chunks(pe, pair)

            top_first(slice(batch - SAMPLES, batch), chunks)
            pe.wait_ge(kept2_summed, chunks)
            for t in range(tiles1):
                nc.tensor.matmul(mlp[t][:, 0:batch], top1_sb[:, 1, P * t:P * (t + 1)], sums2[:],
                                 start=False, stop=True).then_inc(hid1_acc, 1)
            for t in range(tiles2):
                for k in range(tiles1):
                    pe.wait_ge(hid1_ready, k + 1)
                    last = nc.tensor.matmul(y[t][:, 0:batch], top2_sb[:, k, P * t:P * (t + 1)], hid1[:, k, :],
                                            start=k == 0, stop=k == tiles1 - 1)
                last.then_inc(hid2_acc, 1)
            for k in range(tiles2):
                pe.wait_ge(hid2_ready, k + 1)
                last = nc.tensor.matmul(y[2][0:1, 0:batch], top3_sb[:, k:k + 1], hid2[:, k, :],
                                        start=k == 0, stop=k == tiles2 - 1)
            last.then_inc(score_acc, 1)

        @block.scalar
        def _(act):
            def relu(dst, src, bias):
                return nc.scalar.activation(dst, src, ACT.Relu, bias=bias)

            def round_high(dst, src):
                return nc.scalar.activation(dst, src, ACT.Copy)

            def make_high(layer, c, u, k, start):
                act.wait_ge(whole_made, split_number(layer, c, k) + 1)
                if not (start and split_number(layer, c, k) < SPLIT_RING):
                    act.wait_ge(split_used, split_number(layer, c, k) - SPLIT_RING + 1)
                slot = split_slot(layer, u, k)
                round_high(z_high[:, slot, :, :], z_whole[:, slot, :, :]).then_inc(high_made, 1)

            def make_rest_high(c, parts):
                if 0 in parts:
                    act.wait_ge(rest_made, c + 1)
                    if not fixed(c, 0):
                        act.wait_ge(rest_used, c)
                for part in parts:
                    round_high(rest_parts[FIELDS * part:FIELDS * (part + 1), :],
                               rest_whole[:]).then_inc(rest_high, 1)

            def evacuate(layer, c, u, rest_of=None):
                if layer == 0:
                    act.wait_ge(rest_used, c + 1)
                else:
                    act.wait_ge(plain_used, plain_number(1, c, UNITS))
                up = slice(HALF, P)
                bias = bias_sb[up, layer:layer + 1]
                relu(h[layer][up, :], y[layer][up, :], bias).then_inc(h_ready[layer], 1)
                relu(h[layer][0:HALF, :], y[layer][up, :], bias).then_inc(h_ready[layer], 1)
                if rest_of is not None:
                    make_rest_high(rest_of, (1, 2))
                if layer == 0 and not (fixed(c, 0) or fixed(c, 1)):
                    act.wait_ge(kept01_summed, c - 1)
                relu(kept01[HALF * layer:HALF * (layer + 1), u, :], y[layer][0:HALF, :],
                     bias_sb[0:HALF, layer:layer + 1]).then_inc(kept_ready[layer], 1)

            def evacuate2(c):
                act.wait_ge(plain_used, plain_number(2, c, UNITS))
                if not fixed(c, 0):
                    act.wait_ge(kept2_summed, c)
                relu(kept2[:], y[2][:], bias_sb[:, 2:3]).then_inc(kept_ready[2], 1)

            def pair(c0, n, first, last):
                for u in range(2):
                    c = c0 + u
                    start = first and u == 0
                    end = last and u == 1
                    for j, k in enumerate(sorted(SPLIT)):
                        make_high(1, c, u, k, start)
                        if j == 1 and not start:
                            evacuate2(c - 1)
                    if not end:
                        make_rest_high(c + 1, (0,))
                    evacuate(1, c, u, None if end else c + 1)
                    for j, k in enumerate(sorted(SPLIT)):
                        make_high(2, c, u, k, False)
                        if j == 1 and not end:
                            evacuate(0, c + 1, 1 - u)

            act.wait_ge(w0_loaded, 16 * 5)
            round_high(w_rest_parts[:], w_rest[:]).then_inc(w_high_ready, 1)
            for layer in (1, 2):
                act.wait_ge(w_loaded[layer], 32)
                for j, k in enumerate(sorted(SPLIT)):
                    round_high(w_high[layer][:, j, :, :],
                               w_whole[layer][:, j, :, :]).then_inc(w_high_ready, 1)
            act.wait_ge(bias_loaded, 16)
            make_rest_high(0, (0, 1, 2))
            evacuate(0, 0, 0)
            over_chunks(act, pair)
            evacuate2(chunks - 1)
            act.wait_ge(top_loaded, 16 * TOP_DMAS)
            for t in range(tiles1):
                act.wait_ge(hid1_acc, t + 1)
                relu(hid1[:, t, :], mlp[t][:, 0:batch], top1_bias_sb[:, t:t + 1]).then_inc(hid1_ready, 1)
            for t in range(tiles2):
                act.wait_ge(hid2_acc, t + 1)
                relu(hid2[:, t, :], y[t][:, 0:batch], top2_bias_sb[:, t:t + 1]).then_inc(hid2_ready, 1)


_INS = ["ids", "table", "w0a", "w0b", "w0_rest", "w1", "w2", "biases", "dense",
        "top1", "top1_bias", "top2", "top2_bias", "top3"]


def _laid_out(inputs):
    import numpy as np

    f = {k: np.asarray(v) for k, v in inputs.items()}
    a = {}
    tables = [f[f"tbl_{i}"] for i in range(FIELDS)]
    starts = np.cumsum([0] + [t.shape[0] for t in tables[:-1]])
    batch = f["ids"].shape[0]
    chunks = batch // SAMPLES
    rows = f["ids"].T.reshape(FIELDS, chunks, QUARTER, LOOKUPS).transpose(0, 2, 1, 3).reshape(P, -1)
    offsets = np.repeat(starts.astype(rows.dtype), QUARTER * LOOKUPS).reshape(P, LOOKUPS)
    a["ids"] = np.concatenate([rows, offsets], axis=1)
    a["table"] = np.concatenate(tables, axis=0)
    w0 = f["L0_rec_W0"].reshape(P, FIELDS, FIELDS)
    g, k, t = np.meshgrid(np.arange(FIELDS), np.arange(QUARTER), np.arange(PAIR_TILES), indexing="ij")
    other = (g + PAIR_TILES * k + t) % FIELDS
    a["w0a"] = w0[:, g, other].reshape(P, P, PAIR_TILES).transpose(1, 2, 0)
    w0b = w0[:, other, g]
    w0b[:, :, 0, 0] = 0
    a["w0b"] = w0b.reshape(P, P, PAIR_TILES).transpose(1, 2, 0)
    g = np.arange(FIELDS)
    a["w0_rest"] = w0[:, g, (g + FIELDS // 2) % FIELDS].T
    for i in (1, 2):
        w = f[f"L0_rec_W{i}"].reshape(P, UNITS, UNIT, P).transpose(3, 1, 2, 0)
        a[f"w{i}"] = w[:, [k for k in range(UNITS) if k not in SPLIT] + sorted(SPLIT)]
    a["biases"] = np.stack([f[f"L0_rec_b{i}"] for i in range(3)], axis=1)
    a["dense"] = f["dense_ctx"].T
    a["top1"] = f["W_top1"]
    a["top1_bias"] = f["b_top1"].reshape(-1, P).T
    a["top2"] = f["W_top2"].reshape(-1, P, f["W_top2"].shape[1]).transpose(1, 0, 2)
    a["top2_bias"] = f["b_top2"].reshape(-1, P).T
    a["top3"] = f["W_top3"].reshape(-1, P).T
    return {k: np.ascontiguousarray(v) for k, v in a.items()}


def kernel(**inputs):
    import numpy as np
    import concourse.bacc as bacc
    from concourse.bass_utils import run_bass_kernel_spmd

    laid = _laid_out(inputs)
    batch = np.asarray(inputs["ids"]).shape[0]
    nc = bacc.Bacc("TRN2", target_bir_lowering=False, num_devices=1)
    args = [nc.dram_tensor(name, laid[name].shape, mybir.dt.from_np(laid[name].dtype),
                           kind="ExternalInput").ap() for name in _INS]
    out = nc.dram_tensor("score", (1, batch), F32, kind="ExternalOutput").ap()
    cin_tower(nc, *args, out)
    r = run_bass_kernel_spmd(nc, [{name: laid[name] for name in _INS}], core_ids=[0])
    return r.results[0]["score"].reshape(batch, 1)
```
